# Optimizing a Trainium2 kernel written in Bass

```python
import numpy as np
import jax
import jax.numpy as jnp

def _softmax(x, axis=-1):
    return jax.nn.softmax(x, axis=axis)

def _gelu(x):
    return jax.nn.gelu(x, approximate=True)

def _silu(x):
    return jax.nn.silu(x)

def _sigmoid(x):
    return jax.nn.sigmoid(x)

def _layernorm(x, axis=-1, eps=1e-05):
    m = jnp.mean(x, axis=axis, keepdims=True)
    v = jnp.var(x, axis=axis, keepdims=True)
    return (x - m) / jnp.sqrt(v + eps)

def _scatter_add(tgt, idx, src, axis=0):
    return tgt.at[idx].add(src)

def _segment_sum(src, seg, n):
    return jax.ops.segment_sum(src, seg, n)
kernel_name = 'mk_adj_resnorm_d4_adj_r2_c8e243'

def setup_inputs(seed: int=0):
    np.random.seed(seed)
    _w = jnp.asarray

    def _rec_inputs():
        import jax
        import jax.numpy as jnp
        _gk = jax.random.key(seed)
        x = -0.000929 + 1 * jax.random.normal(jax.random.fold_in(_gk, 1), (4096, 64), jnp.float32)
        _a = jax.random.bernoulli(jax.random.fold_in(_gk, 2), 0.000976562, (4096, 4096))
        _a = jnp.logical_or(_a, jnp.swapaxes(_a, -1, -2))
        _a = jnp.logical_or(_a, jnp.eye(4096, dtype=bool))
        _af = _a.astype(jnp.float32)
        _af = _af * jax.random.uniform(jax.random.fold_in(_gk, 3), (4096, 4096), jnp.float32, 0.05, 1)
        adj = _af
        return (x, adj)
    x, adj = _rec_inputs()

    def _L0_gnn_setup():
        import jax, jax.numpy as jnp
        import numpy as np
        N = 8192
        F_IN = 64
        F_OUT = 64
        key = jax.random.key(seed)
        k1, k2, k3 = jax.random.split(key, 3)
        inp = jax.random.normal(k1, (N, F_IN), dtype=jnp.float32)
        adj = jax.random.uniform(k2, (N, N), dtype=jnp.float32)
        limit = np.sqrt(6.0 / (F_IN + F_OUT)).astype(np.float32)
        W = jax.random.uniform(k3, (F_IN, F_OUT), dtype=jnp.float32, minval=-limit, maxval=limit)
        b = jnp.zeros((F_OUT,), dtype=jnp.float32)
        return {'input': inp, 'adj': adj, 'W': W, 'b': b}
    _L0_gnn_all = _L0_gnn_setup()
    _L0_gnn_in = {k: v for k, v in _L0_gnn_all.items() if k in ('W', 'b')}
    del _L0_gnn_all

    def _L1_gnn_setup():
        import jax, jax.numpy as jnp
        import numpy as np
        N = 8192
        D_IN = 64
        D_OUT = 64
        EDGE_P = 0.002
        key = jax.random.key(seed)
        kx, ka, kw = jax.random.split(key, 3)
        X = jax.random.normal(kx, (N, D_IN), dtype=jnp.float32)
        adj = (jax.random.uniform(ka, (N, N)) < EDGE_P).astype(jnp.float32)
        W = jax.random.normal(kw, (D_OUT, 2 * D_IN), dtype=jnp.float32) * (1.0 / np.sqrt(2 * D_IN))
        return {'X': X, 'adj': adj, 'W': W}
    _L1_gnn_all = _L1_gnn_setup()
    _L1_gnn_in = {k: v for k, v in _L1_gnn_all.items() if k in ('W',)}
    del _L1_gnn_all

    def _L2_gnn_setup():
        import jax, jax.numpy as jnp
        import numpy as np
        N = 2048
        D = 64
        NUM_LAYERS = 2
        THETA0 = 0.000244
        THETA_MAX = 0.0003
        LAM = 0.1
        TAU = 1.0
        EPS = 1e-06
        H_DENSITY = 0.005

        def _safe_norm(x, axis):
            return jnp.sqrt(jnp.maximum(jnp.sum(x * x, axis=axis), 1e-16))

        def _layer(x, H, W, Theta, Wq, bq, Wv, bv, iteration):
            scale = D ** (-0.5)
            theta_base = THETA0 + (1.0 - np.exp(-LAM * iteration)) * (THETA_MAX - THETA0)
            th_comp = theta_base
            th_edge = min(theta_base, 0.8)
            th_node = min(theta_base, 0.7)
            structural = _safe_norm(x @ W, axis=1)
            Q = x @ Wq + bq
            V = x @ Wv + bv
            edge_feat = H.T @ V
            att = Q @ edge_feat.T * scale * H
            att = jax.nn.softmax(att, axis=1)
            att_scores = att.mean(axis=0)
            importance = 0.5 * structural + 0.5 * att_scores
            comp_scores = jax.nn.softmax(importance / TAU)
            comp_mask = comp_scores >= th_comp
            x_comp = x * comp_mask[:, None]
            nrm = jnp.maximum(_safe_norm(x_comp, axis=1), 1e-08)
            xn = x_comp / nrm[:, None]
            cos = xn @ xn.T
            edge_scores = jax.nn.softmax(cos * H / TAU, axis=1)
            edge_mask = (edge_scores >= th_edge) & comp_mask[:, None]
            H_pruned = H * edge_mask
            connectivity = H_pruned.sum(axis=1)
            feat_mag = _safe_norm(x_comp, axis=1)
            node_scores = jax.nn.softmax(connectivity * feat_mag / TAU)
            connected = (H_pruned * edge_mask).sum(axis=1) > 0
            node_mask = (node_scores >= th_node) & connected
            x_final = x_comp * node_mask[:, None]
            vdeg = jnp.maximum(H_pruned.sum(axis=1), EPS)
            edeg = jnp.maximum(H_pruned.sum(axis=0), EPS)
            dv_isqrt = 1.0 / jnp.sqrt(vdeg)
            de_inv = 1.0 / edeg
            transformed = x_final @ W
            agg = H_pruned.T * dv_isqrt[None, :] @ transformed
            agg = agg * de_inv[:, None]
            msg = dv_isqrt[:, None] * (H_pruned @ agg)
            msg = msg @ Theta
            return jax.nn.relu(msg)
        key = jax.random.key(seed)
        ks = jax.random.split(key, 8)
        xav = 0.125
        X = jax.random.normal(ks[0], (N, D), jnp.float32) * 0.05
        W = jax.random.normal(ks[1], (D, D), jnp.float32) * xav
        Theta = jax.random.normal(ks[2], (D, D), jnp.float32) * xav
        Wq = jax.random.normal(ks[3], (D, D), jnp.float32) * xav
        bq = jnp.zeros((D,), jnp.float32)
        Wv = jax.random.normal(ks[4], (D, D), jnp.float32) * xav
        bv = jnp.zeros((D,), jnp.float32)
        H = (jax.random.uniform(ks[7], (N, N)) < H_DENSITY).astype(jnp.float32)
        return {'X': X, 'W': W, 'Theta': Theta, 'Wq': Wq, 'bq': bq, 'Wv': Wv, 'bv': bv, 'H': H}
    _L2_gnn_all = _L2_gnn_setup()
    _L2_gnn_in = {k: v for k, v in _L2_gnn_all.items() if k in ('W', 'Theta', 'Wq', 'bq', 'Wv', 'bv')}
    del _L2_gnn_all

    def _L3_gnn_setup():
        import jax, jax.numpy as jnp
        import numpy as np
        N, D_IN, D_OUT = (4096, 64, 64)
        MAX_NEIGH = 100
        DECAY = 0.5
        key = jax.random.key(seed)
        k1, k2, k3, k4 = jax.random.split(key, 4)
        stdv = 1.0 / np.sqrt(D_OUT)
        inputs = {'input': jax.random.normal(k1, (N, D_IN), dtype=jnp.float32), 'adj': jax.random.randint(k2, (N, N), 0, 2).astype(jnp.float32), 'weight': jax.random.uniform(k3, (D_IN, D_OUT), minval=-stdv, maxval=stdv, dtype=jnp.float32), 'bias': jax.random.uniform(k4, (D_OUT,), minval=-stdv, maxval=stdv, dtype=jnp.float32)}
        return inputs
    _L3_gnn_all = _L3_gnn_setup()
    _L3_gnn_in = {k: v for k, v in _L3_gnn_all.items() if k in ('weight', 'bias')}
    del _L3_gnn_all
    return {'x': x, 'adj': adj, 'L0_gnn_W': _L0_gnn_in['W'], 'L0_gnn_b': _L0_gnn_in['b'], 'L1_gnn_W': _L1_gnn_in['W'], 'L2_gnn_W': _L2_gnn_in['W'], 'L2_gnn_Theta': _L2_gnn_in['Theta'], 'L2_gnn_Wq': _L2_gnn_in['Wq'], 'L2_gnn_bq': _L2_gnn_in['bq'], 'L2_gnn_Wv': _L2_gnn_in['Wv'], 'L2_gnn_bv': _L2_gnn_in['bv'], 'L3_gnn_weight': _L3_gnn_in['weight'], 'L3_gnn_bias': _L3_gnn_in['bias']}

def reference(x, adj, L0_gnn_W, L0_gnn_b, L1_gnn_W, L2_gnn_W, L2_gnn_Theta, L2_gnn_Wq, L2_gnn_bq, L2_gnn_Wv, L2_gnn_bv, L3_gnn_weight, L3_gnn_bias):
    import jax
    import jax.numpy as jnp

    def _L0_gnn_ref(input, adj, W, b):
        import jax, jax.numpy as jnp
        import numpy as np
        N = 8192
        F_IN = 64
        F_OUT = 64
        h = input @ W
        out = adj @ h + b
        return out

    def _L1_gnn_ref(X, adj, W):
        import jax, jax.numpy as jnp
        import numpy as np
        N = 8192
        D_IN = 64
        D_OUT = 64
        EDGE_P = 0.002
        deg = jnp.sum(adj, axis=1, keepdims=True)
        nb_agg = adj @ X / jnp.maximum(deg, 1.0)
        X_cat = jnp.concatenate([X, nb_agg], axis=1)
        out = X_cat @ W.T
        return jax.nn.relu(out)

    def _L2_gnn_ref(X, W, Theta, Wq, bq, Wv, bv, H):
        import jax, jax.numpy as jnp
        import numpy as np
        N = 2048
        D = 64
        NUM_LAYERS = 2
        THETA0 = 0.000244
        THETA_MAX = 0.0003
        LAM = 0.1
        TAU = 1.0
        EPS = 1e-06
        H_DENSITY = 0.005

        def _safe_norm(x, axis):
            return jnp.sqrt(jnp.maximum(jnp.sum(x * x, axis=axis), 1e-16))

        def _layer(x, H, W, Theta, Wq, bq, Wv, bv, iteration):
            scale = D ** (-0.5)
            theta_base = THETA0 + (1.0 - np.exp(-LAM * iteration)) * (THETA_MAX - THETA0)
            th_comp = theta_base
            th_edge = min(theta_base, 0.8)
            th_node = min(theta_base, 0.7)
            structural = _safe_norm(x @ W, axis=1)
            Q = x @ Wq + bq
            V = x @ Wv + bv
            edge_feat = H.T @ V
            att = Q @ edge_feat.T * scale * H
            att = jax.nn.softmax(att, axis=1)
            att_scores = att.mean(axis=0)
            importance = 0.5 * structural + 0.5 * att_scores
            comp_scores = jax.nn.softmax(importance / TAU)
            comp_mask = comp_scores >= th_comp
            x_comp = x * comp_mask[:, None]
            nrm = jnp.maximum(_safe_norm(x_comp, axis=1), 1e-08)
            xn = x_comp / nrm[:, None]
            cos = xn @ xn.T
            edge_scores = jax.nn.softmax(cos * H / TAU, axis=1)
            edge_mask = (edge_scores >= th_edge) & comp_mask[:, None]
            H_pruned = H * edge_mask
            connectivity = H_pruned.sum(axis=1)
            feat_mag = _safe_norm(x_comp, axis=1)
            node_scores = jax.nn.softmax(connectivity * feat_mag / TAU)
            connected = (H_pruned * edge_mask).sum(axis=1) > 0
            node_mask = (node_scores >= th_node) & connected
            x_final = x_comp * node_mask[:, None]
            vdeg = jnp.maximum(H_pruned.sum(axis=1), EPS)
            edeg = jnp.maximum(H_pruned.sum(axis=0), EPS)
            dv_isqrt = 1.0 / jnp.sqrt(vdeg)
            de_inv = 1.0 / edeg
            transformed = x_final @ W
            agg = H_pruned.T * dv_isqrt[None, :] @ transformed
            agg = agg * de_inv[:, None]
            msg = dv_isqrt[:, None] * (H_pruned @ agg)
            msg = msg @ Theta
            return jax.nn.relu(msg)
        x = X
        for it in range(NUM_LAYERS):
            x = _layer(x, H, W, Theta, Wq, bq, Wv, bv, it)
        return x

    def _L3_gnn_ref(input, adj, weight, bias):
        import jax, jax.numpy as jnp
        import numpy as np
        N, D_IN, D_OUT = (4096, 64, 64)
        MAX_NEIGH = 100
        DECAY = 0.5
        support = input @ weight
        mask = (adj != 0).astype(support.dtype)
        rank = jnp.cumsum(mask, axis=1)
        deg = rank[:, -1:]
        k = jnp.minimum(deg, float(MAX_NEIGH))
        pos = rank - (deg - k)
        w = mask * jnp.where(pos > 0, DECAY ** (k - pos), 0.0)
        out = w @ support + bias
        return out
    x = _layernorm(x + _L0_gnn_ref(x, adj, L0_gnn_W, L0_gnn_b), axis=-1)
    x = _layernorm(x + _L1_gnn_ref(x, adj, L1_gnn_W), axis=-1)
    x = _layernorm(x + _L2_gnn_ref(x, L2_gnn_W, L2_gnn_Theta, L2_gnn_Wq, L2_gnn_bq, L2_gnn_Wv, L2_gnn_bv, adj), axis=-1)
    x = _layernorm(x + _L3_gnn_ref(x, adj, L3_gnn_weight, L3_gnn_bias), axis=-1)
    return x

_drawn_inputs = setup_inputs


def setup_inputs(seed=0):
    import zlib

    import numpy as np

    out = dict(_drawn_inputs(seed))
    spreads = {'L0_gnn_b': (0.0, 0.1), 'L2_gnn_bq': (0.0, 0.1), 'L2_gnn_bv': (0.0, 0.1)}
    factors = {}
    for name, (base, spread) in spreads.items():
        noise = np.random.default_rng([zlib.crc32(name.encode()), seed]).standard_normal(out[name].shape)
        drawn = base * np.exp(spread * noise) if base else spread * noise
        out[name] = jnp.asarray(drawn.astype(out[name].dtype))
    for name, factor in factors.items():
        out[name] = (out[name] * factor).astype(out[name].dtype)
    return out
```

```python
import concourse.bass as bass
from concourse import mybir
from contextlib import ExitStack, contextmanager
import numpy as np

F32 = mybir.dt.float32
BF16 = mybir.dt.bfloat16
ALU = mybir.AluOpType
ACT = mybir.ActivationFunctionType
AX = mybir.AxisListType

P = 128
N = 4096
F = 64
NB = N // P
HALF = N // 2
HB = NB // 2
BANK = 512
LN_EPS = 1e-5
DEG_EPS = 1e-6
NORM_FLOOR = 1e-16
NEG_HUGE = -3.0e38
REFUSE = 1.0e30
W_FLOOR = 2.0 ** -100
THETAS = [0.000244 + (1.0 - float(np.exp(-0.1 * it))) * (0.0003 - 0.000244) for it in range(2)]


class Step:

    def __init__(self, n, k, it, unroll):
        self.n, self.k, self.it, self.unroll = n, k, it, unroll

    def slot(self, slots):
        return self.k % slots

    def turn(self, slots):
        if self.it is None:
            return self.k // slots
        assert self.unroll % slots == 0
        return self.it * (self.unroll // slots) + self.k // slots


def row_blocks(e, unroll, lead, tail, body):
    groups = (NB - lead - tail) // unroll
    assert lead + tail + groups * unroll == NB
    for n in range(lead):
        body(Step(n, n, None, unroll))
    with e.Fori(0, groups) as it:
        for u in range(unroll):
            body(Step(it * unroll + (lead + u), lead + u, it, unroll))
    for n in range(NB - tail, NB):
        body(Step(n, n, None, unroll))


def wait(e, sem, value):
    if isinstance(value, int) and value <= 0:
        return
    e.wait_ge(sem, value)


def build(nc, d):
    ctx = ExitStack()
    with ctx:
        def sb(name, shape, dt=F32):
            return ctx.enter_context(nc.sbuf_tensor(name, shape, dt))

        ps = ctx.enter_context(nc.psum_tensor("ps", [P, 8, BANK], F32))
        res = sb("res", [P, NB, F])
        cur = sb("cur", [P, NB, F])
        moved = sb("moved", [P, NB, F])
        xw = sb("xw", [P, NB, F])
        tmp = sb("tmp", [P, NB, F])
        accT = sb("accT", [P, HALF])
        curT = sb("curT", [P, HALF])
        rows = sb("rows", [P, 2 * BANK])
        mov_a = sb("mov_a", [P, N], BF16)
        mov_b = sb("mov_b", [P, N], BF16)
        mov_c = sb("mov_c", [P, N], BF16)
        sta_a = sb("sta_a", [P, N], BF16)
        sta_b = sb("sta_b", [P, N], BF16)
        stage = sb("stage", [P, 4, F])
        ident = sb("ident", [P, P])
        ident_b = sb("ident_b", [P, P], BF16)
        neg_ident_b = sb("neg_ident_b", [P, P], BF16)
        ones = sb("ones", [P, 1])
        zeros_b = sb("zeros_b", [P, BANK], BF16)
        floor_w = sb("floor_w", [P, 1])
        w0, w1s, w1n, wq, theta, w3 = (sb(n, [P, F]) for n in ("w0", "w1s", "w1n", "wq", "theta", "w3"))
        wvw = sb("wvw", [P, 2 * F])
        b0, bv, b3 = (sb(n, [P, F]) for n in ("b0", "bv", "b3"))
        bq8 = sb("bq8", [P, 1])
        st = {n: sb(n, [P, NB]) for n in ("mean", "var", "std", "rdeg", "struct", "sumsq", "comp", "feat",
                                          "refuse", "conn", "dv", "score", "node")}
        gl = {n: sb(n, [P, 1]) for n in ("gmax", "gmaxall", "gneg", "gsum", "gsumall", "grec")}
        mx4 = sb("mx4", [P, 3, 4])
        negmax = sb("negmax", [P, 3])
        zsum = sb("zsum", [P, 3])
        rz = sb("rz", [P, 3])
        cut = sb("cut", [P, 3])
        msgT = sb("msgT", [P, 2, P])
        stream = sb("stream", [P, 6, N])
        streamb = stream[:, 4:6, :].rearrange("p s n -> p (s n)").bitcast(BF16)

        Hp = nc.dram_tensor("pruned", (N, N), F32, kind="Internal").ap()

        def by_rows(m):
            return m.rearrange("(n p) c -> n p c", p=P)

        adj_b, adjT_b, Hp_b = by_rows(d["adj"]), by_rows(d["adjT"]), by_rows(Hp)

        @contextmanager
        def phase(name):
            made = []

            def sem(n):
                s = nc.alloc_semaphore(f"{name}_{n}")
                made.append(s)
                return s

            with nc.Block() as block:
                yield block, sem
            nc.clear_and_free_semaphores(made)
            nc.all_engine_barrier()

        nat4 = ps[:, 0:4, :].rearrange("p b (k f) -> p (b k) f", f=F)
        nat4b = ps[:, 4:8, :].rearrange("p b (k f) -> p (b k) f", f=F)
        wide = ps[:, :, :].rearrange("p b (k f) -> p (b k) f", f=2 * F)
        fold4 = ps[:, 0:4, :].rearrange("p b c -> p (b c)")
        full = ps[:, :, :].rearrange("p b c -> p (b c)")

        def per_node(a):
            return a[:, :].unsqueeze(2).to_broadcast([P, NB, F])

        def per_feature(a):
            return a[:, :].unsqueeze(1).to_broadcast([P, NB, F])

        def project(dst, srcT, w):
            for b in range(NB):
                r = F * (b // HB)
                c = P * (b % HB)
                last = nc.tensor.matmul(dst[:, b, :], srcT[r:r + F, c:c + P], w[r:r + F, :], start=True, stop=True)
            return last

        def fold(src):
            for c in range(HB):
                for h in range(2):
                    last = nc.tensor.matmul(fold4[F * h:F * h + F, P * c:P * c + P], src[:, HB * h + c, :],
                                            ident[:, :], start=True, stop=True)
            return last

        def twice(src):
            for b in range(NB):
                for h in range(2):
                    last = nc.tensor.matmul(full[F * h:F * h + F, P * b:P * b + P], src[:, b, :],
                                            ident[:, :], start=True, stop=True)
            return last

        def twice_folded(srcT, w):
            for b in range(8):
                r = F * (b // 4)
                for h in range(2):
                    last = nc.tensor.matmul(ps[F * h:F * h + F, b, :], w[r:r + F, 0:F],
                                            srcT[r:r + F, BANK * (b % 4):BANK * (b % 4) + BANK],
                                            start=True, stop=True)
            return last

        def rows_to_columns(bank):
            for b in range(NB):
                chunk, off = divmod(P * b, BANK)
                g, j = chunk % 4, chunk // 4
                at = 4 * j + b % 4
                last = nc.tensor.matmul(ps[:, bank + g, at:at + 1],
                                        rows[32 * g:32 * g + 1, BANK * j + off:BANK * j + off + P],
                                        ones[32 * g:32 * g + 1, :], start=True, stop=True)
            return last

        def columns(bank):
            return ps[:, bank:bank + 4, 0:8].rearrange("p g (j i) -> p j g i", i=4)

        def blocks4(a):
            return a[:, :].rearrange("p (j g i) -> p j g i", j=2, g=4)

        class Chain:

            def __init__(self, e, sem):
                self.e, self.sem, self.count = e, sem, 0

            def __call__(self, ins):
                self.count += 1
                ins.then_inc(self.sem, 1)
                self.e.wait_ge(self.sem, self.count)

        def layer_norm(dve, do, dst, y, var_ready, std_ready):
            v = nc.vector
            do(v.reduce_sum(st["mean"][:, :], y[:, :, :], AX.X))
            do(v.tensor_scalar(st["mean"][:, :], st["mean"][:, :], 1.0 / F, None, ALU.mult))
            do(v.tensor_tensor(y[:, :, :], y[:, :, :], per_node(st["mean"]), ALU.subtract))
            do(v.tensor_tensor(tmp[:, :, :], y[:, :, :], y[:, :, :], ALU.mult))
            do(v.reduce_sum(st["var"][:, :], tmp[:, :, :], AX.X))
            v.tensor_scalar(st["var"][:, :], st["var"][:, :], 1.0 / F, LN_EPS, ALU.mult, ALU.add)\
                .then_inc(var_ready, 1)
            dve.wait_ge(std_ready, 1)
            do(v.reciprocal(st["std"][:, :], st["std"][:, :]))
            do(v.tensor_tensor(dst[:, :, :], y[:, :, :], per_node(st["std"]), ALU.mult))

        def root_of_variance(act, var_ready, std_ready):
            act.wait_ge(var_ready, 1)
            nc.scalar.activation(st["std"][:, :], st["var"][:, :], ACT.Sqrt).then_inc(std_ready, 1)

        def split(do, stationary, moving):
            v = nc.vector
            rest = stream[:, 0, :]
            hi, mid, lo = (streamb[:, N * i:N * i + N] for i in range(3))
            do(v.tensor_copy(hi, full))
            do(v.tensor_tensor(rest, full, hi, ALU.subtract))
            do(v.tensor_copy(mid, rest))
            do(v.tensor_tensor(lo, rest, mid, ALU.subtract))
            top, low = slice(0, F), slice(F, P)
            if stationary:
                do(v.tensor_copy(sta_a[top, :], hi[top, :]))
                do(v.tensor_copy(sta_a[low, :], mid[low, :]))
                do(v.tensor_copy(sta_b[top, :], hi[top, :]))
                do(v.tensor_copy(sta_b[low, :], lo[low, :]))
            if moving:
                do(v.tensor_copy(mov_a[:, :], hi))
                do(v.tensor_copy(mov_b[:, :], mid))
                do(v.tensor_copy(mov_c[top, :], lo[top, :]))
                do(v.tensor_copy(mov_c[low, :], hi[low, :]))

        def accumulate(name, matrix_b, column_sums):
            SL = 4
            with phase(name) as (block, sem):
                loaded = [sem(f"block_loaded{s}") for s in range(SL)]
                staged = sem("stationary_staged")
                used = sem("block_used")

                @block.sync
                def _(sp):
                    def body(t):
                        wait(sp, used, t.n - (SL - 1))
                        sp.dma_start(stream[:, t.slot(SL), :], matrix_b[t.n]).then_inc(loaded[t.slot(SL)], 16)
                    row_blocks(sp, SL, SL, 0, body)

                @block.scalar
                def _(act):
                    def body(t):
                        wait(act, used, t.n - (SL - 1))
                        src = moved[:, t.n, :] if isinstance(t.n, int) else \
                            moved[:, bass.ds(t.n, 1), :].rearrange("p a f -> p (a f)")
                        nc.scalar.activation(stage[:, t.slot(SL), :], src, ACT.Copy).then_inc(staged, 1)
                    row_blocks(act, SL, SL, 0, body)

                @block.tensor
                def _(pe):
                    for b in range(4):
                        for h in range(2):
                            nc.tensor.matmul(ps[F * h:F * h + F, b, :], zeros_b[:, 0:F], zeros_b[:, :],
                                             start=True, stop=False, skip_group_check=True)
                    if column_sums:
                        for c in range(8):
                            g, j = c % 4, c // 4
                            nc.tensor.matmul(ps[32 * g:32 * g + 1, 4 + j, :], zeros_b[:, 0:1], zeros_b[:, :],
                                             start=True, stop=False, skip_group_check=True)

                    def body(t):
                        s = t.slot(SL)
                        pe.wait_ge(loaded[s], 16 * (t.turn(SL) + 1))
                        pe.wait_ge(staged, t.n + 1)
                        for b in range(4):
                            for h in range(2):
                                c = HALF * h + BANK * b
                                last = nc.tensor.matmul(ps[F * h:F * h + F, b, :], stage[:, s, :],
                                                        stream[:, s, c:c + BANK], start=False, stop=False,
                                                        skip_group_check=True)
                        if column_sums:
                            for c in range(8):
                                g, j = c % 4, c // 4
                                last = nc.tensor.matmul(ps[32 * g:32 * g + 1, 4 + j, :], ones[:, :],
                                                        stream[:, s, BANK * c:BANK * c + BANK], start=False,
                                                        stop=False, skip_group_check=True)
                        last.then_inc(used, 1)
                    row_blocks(pe, SL, SL, 0, body)

        def take_rows(act, base, taken):
            for g in range(4):
                nc.scalar.activation(rows[32 * g:32 * g + 1, :],
                                     ps[32 * g:32 * g + 1, base:base + 2, :].rearrange("p a b -> p (a b)"),
                                     ACT.Copy).then_inc(taken, 1)

        with phase("setup") as (block, sem):
            small_loaded, ident_zero, ident_made = sem("small_loaded"), sem("ident_zero"), sem("ident_made")
            const_made, h_ready, chain = sem("const_made"), sem("h_ready"), sem("dve_step")
            loads = [(res[:, :, :], d["x"].rearrange("(n p) f -> p n f", p=P)),
                     (wvw[0:F, 0:F], d["Wv"]), (wvw[F:P, 0:F], d["Wv"]),
                     (wvw[0:F, F:P], d["W"]), (wvw[F:P, F:P], d["W"])]
            for h in range(2):
                r = slice(F * h, F * h + F)
                loads += [(curT[r, :], d["xT"][:, HALF * h:HALF * h + HALF]),
                          (w0[r, :], d["W0"]), (w1s[r, :], d["W1T"][0:F, :]), (w1n[r, :], d["W1T"][F:P, :]),
                          (wq[r, :], d["Wq"]), (theta[r, :], d["Theta"]), (w3[r, :], d["W3"]),
                          (bq8[r, :], d["bq"].rearrange("(f a) -> f a", a=1))]
            for t, n in ((b0, "b0"), (bv, "bv"), (b3, "b3")):
                loads += [(t[:, :], d[n].rearrange("(a f) -> a f", a=1).broadcast_to([P, F]))]

            @block.sync
            def _(sp):
                for dst, src in loads:
                    sp.dma_start(dst, src).then_inc(small_loaded, 16)

            @block.gpsimd
            def _(pool):
                nc.gpsimd.memset(ident[:, :], 0.0).then_inc(ident_zero, 1)
                pool.wait_ge(ident_zero, 1)
                nc.gpsimd.affine_select(out=ident[:, :], in_=ident[:, :], compare_op=ALU.not_equal, fill=1.0,
                                        base=0, pattern=[[-1, P]], channel_multiplier=1).then_inc(ident_made, 1)

            @block.tensor
            def _(pe):
                pe.wait_ge(small_loaded, 16 * len(loads))
                project(nat4, curT, w0).then_inc(h_ready, 1)

            @block.vector
            def _(dve):
                v = nc.vector
                do = Chain(dve, chain)
                do(v.memset(ones[:, :], 1.0))
                do(v.memset(zeros_b[:, :], 0.0))
                do(v.memset(floor_w[:, :], W_FLOOR))
                dve.wait_ge(ident_made, 1)
                do(v.tensor_copy(ident_b[:, :], ident[:, :]))
                do(v.tensor_scalar(neg_ident_b[:, :], ident[:, :], -1.0, None, ALU.mult))
                dve.wait_ge(small_loaded, 16 * len(loads))
                do(v.tensor_scalar(bq8[:, :], bq8[:, :], 0.125, None, ALU.mult))
                dve.wait_ge(h_ready, 1)
                do(v.tensor_copy(moved[:, :, :], nat4))

        accumulate("l0", adjT_b, column_sums=True)

        with phase("l0_end") as (block, sem):
            acc_taken, rows_taken, chain = sem("acc_taken"), sem("rows_taken"), sem("dve_step")
            nat_ready, deg_ready, x_ready, fold_ready = (sem(n) for n in
                                                         ("nat_ready", "deg_ready", "x_ready", "fold_ready"))
            var_ready, std_ready = sem("var_ready"), sem("std_ready")

            @block.scalar
            def _(act):
                take_rows(act, 4, rows_taken)
                root_of_variance(act, var_ready, std_ready)

            @block.tensor
            def _(pe):
                pe.wait_ge(rows_taken, 4)
                rows_to_columns(4).then_inc(deg_ready, 1)
                pe.wait_ge(acc_taken, 1)
                for b in range(NB):
                    h = b // HB
                    last = nc.tensor.matmul(nat4[:, b, :], accT[F * h:F * h + F, P * (b % HB):P * (b % HB) + P],
                                            ident[F * h:F * h + F, F * h:F * h + F], start=True, stop=True)
                last.then_inc(nat_ready, 1)
                pe.wait_ge(x_ready, 1)
                fold(res).then_inc(fold_ready, 1)

            @block.vector
            def _(dve):
                v = nc.vector
                do = Chain(dve, chain)
                v.tensor_copy(accT[:, :], fold4).then_inc(acc_taken, 1)
                do(v.tensor_tensor(res[:, :, :], res[:, :, :], per_feature(b0), ALU.add))
                dve.wait_ge(nat_ready, 1)
                do(v.tensor_tensor(res[:, :, :], nat4, res[:, :, :], ALU.add))
                layer_norm(dve, do, res, res, var_ready, std_ready)
                v.tensor_copy(moved[:, :, :], res[:, :, :]).then_inc(x_ready, 1)
                dve.wait_ge(deg_ready, 1)
                do(v.tensor_scalar(blocks4(st["rdeg"]), columns(4), 1.0, None, ALU.max))
                do(v.reciprocal(st["rdeg"][:, :], st["rdeg"][:, :]))
                dve.wait_ge(fold_ready, 1)
                do(v.tensor_copy(curT[:, :], fold4))

        accumulate("l1", adjT_b, column_sums=False)

        with phase("l1_end") as (block, sem):
            acc_taken, chain, x_ready, fold_ready = (sem(n) for n in
                                                     ("acc_taken", "dve_step", "x_ready", "fold_ready"))
            self_ready, nb_ready = sem("self_ready"), sem("neighbours_ready")
            var_ready, std_ready = sem("var_ready"), sem("std_ready")

            @block.scalar
            def _(act):
                root_of_variance(act, var_ready, std_ready)

            @block.tensor
            def _(pe):
                project(nat4b, curT, w1s).then_inc(self_ready, 1)
                pe.wait_ge(acc_taken, 1)
                project(nat4, accT, w1n).then_inc(nb_ready, 1)
                pe.wait_ge(x_ready, 1)
                fold(res).then_inc(fold_ready, 1)

            @block.vector
            def _(dve):
                v = nc.vector
                do = Chain(dve, chain)
                v.tensor_copy(accT[:, :], fold4).then_inc(acc_taken, 1)
                dve.wait_ge(nb_ready, 1)
                do(v.tensor_tensor(cur[:, :, :], nat4, per_node(st["rdeg"]), ALU.mult))
                dve.wait_ge(self_ready, 1)
                do(v.tensor_tensor(cur[:, :, :], nat4b, cur[:, :, :], ALU.add))
                do(v.scalar_tensor_tensor(out=res[:, :, :].rearrange("p n f -> p (n f)"),
                                          in0=cur[:, :, :].rearrange("p n f -> p (n f)"), scalar=0.0,
                                          in1=res[:, :, :].rearrange("p n f -> p (n f)"),
                                          op0=ALU.max, op1=ALU.add))
                layer_norm(dve, do, res, res, var_ready, std_ready)
                v.tensor_copy(cur[:, :, :], res[:, :, :]).then_inc(x_ready, 1)
                dve.wait_ge(fold_ready, 1)
                do(v.tensor_copy(curT[:, :], fold4))

        def global_softmax_vector(dve, do, sems):
            v = nc.vector
            v.reduce_max(gl["gmax"][:, :], st["score"][:, :], AX.X).then_inc(sems["part_max"], 1)
            dve.wait_ge(sems["all_max"], 1)
            v.tensor_scalar(gl["gneg"][:, :], gl["gmaxall"][:, :], -1.0, None, ALU.mult)\
                .then_inc(sems["bias_ready"], 1)
            dve.wait_ge(sems["all_sum"], 1)
            do(v.reciprocal(gl["grec"][:, :], gl["gsumall"][:, :]))
            do(v.tensor_scalar(st["score"][:, :], st["score"][:, :], gl["grec"][:, :], None, ALU.mult))

        def global_softmax_pool(pool, sems):
            pool.wait_ge(sems["part_max"], 1)
            nc.gpsimd.partition_all_reduce(gl["gmaxall"][:, :], gl["gmax"][:, :], P,
                                           bass.bass_isa.ReduceOp.max).then_inc(sems["all_max"], 1)
            pool.wait_ge(sems["part_sum"], 1)
            nc.gpsimd.partition_all_reduce(gl["gsumall"][:, :], gl["gsum"][:, :], P,
                                           bass.bass_isa.ReduceOp.add).then_inc(sems["all_sum"], 1)

        def global_softmax_scalar(act, sems):
            act.wait_ge(sems["bias_ready"], 1)
            nc.scalar.activation(st["score"][:, :], st["score"][:, :], ACT.Exp, bias=gl["gneg"][:, :],
                                 accum_out=gl["gsum"][:, :]).then_inc(sems["part_sum"], 1)

        SOFT = ("part_max", "all_max", "bias_ready", "part_sum", "all_sum")
        SL3 = 3
        CHUNK = 2 * BANK
        NC = N // CHUNK
        held = [stream[:, s, :] for s in range(3)]
        prod = [stream[:, 3 + s, :] for s in range(3)]

        def score_products(pe, t, scores_ready, chunk_used):
            for c in range(NC):
                slot = (NC * t.k + c) % SL3
                wait(pe, chunk_used, t.n * NC + (c - 2))
                for j in range(2):
                    cols = slice(CHUNK * c + BANK * j, CHUNK * c + BANK * j + BANK)
                    rows_n = bass.ds(t.n * P, P)
                    out = ps[:, 2 * slot + j, :]
                    nc.tensor.matmul(out, sta_a[:, rows_n], mov_a[:, cols], start=True, stop=False)
                    nc.tensor.matmul(out, sta_a[:, rows_n], mov_b[:, cols], start=False, stop=False)
                    last = nc.tensor.matmul(out, sta_b[:, rows_n], mov_c[:, cols], start=False, stop=True)
                last.then_inc(scores_ready, 1)

        def weighted_scores(dve, t, seen, scores_ready, chunk_used, max_ready):
            s = t.slot(SL3)
            for c in range(NC):
                slot = (NC * t.k + c) % SL3
                dve.wait_ge(scores_ready, t.n * NC + (c + 1))
                dve.sem_inc(seen, 1)
                cols = slice(CHUNK * c, CHUNK * c + CHUNK)
                nc.vector.tensor_tensor_reduce(
                    out=prod[s][:, cols], in0=ps[:, 2 * slot:2 * slot + 2, :].rearrange("p a b -> p (a b)"),
                    in1=held[s][:, cols], scale=1.0, scalar=NEG_HUGE, op0=ALU.mult, op1=ALU.max,
                    accum_out=mx4[:, s, c:c + 1]).then_inc(chunk_used, 1)
            dve.wait_ge(chunk_used, t.n * NC + NC)
            nc.vector.tensor_reduce(negmax[:, s:s + 1], mx4[:, s, :], AX.X, ALU.max, negate=True)\
                .then_inc(max_ready, 1)

        def exponentials(act, t, max_ready, exp_done):
            s = t.slot(SL3)
            act.wait_ge(max_ready, t.n + 1)
            nc.scalar.activation(prod[s], prod[s], ACT.Exp, bias=negmax[:, s:s + 1],
                                 accum_out=zsum[:, s:s + 1]).then_inc(exp_done, 1)

        def back(t, by):
            return Step(t.n - by, t.k - by, t.it, t.unroll)

        for it in range(2):
            th = THETAS[it]
            last_it = it == 1

            with phase(f"i{it}_project") as (block, sem):
                vw_ready, vw_taken, q_ready, chain = (sem(n) for n in ("vw_ready", "vw_taken", "q_ready", "dve_step"))
                norm_ready, q_taken, root = sem("norm_ready"), sem("q_taken"), sem("root")

                @block.tensor
                def _(pe):
                    project(wide, curT, wvw).then_inc(vw_ready, 1)
                    pe.wait_ge(vw_taken, 2)
                    twice_folded(curT, wq).then_inc(q_ready, 1)

                @block.scalar
                def _(act):
                    act.wait_ge(vw_taken, 1)
                    nc.scalar.activation(xw[:, :, :], wide[:, :, F:P], ACT.Copy).then_inc(vw_taken, 1)
                    act.wait_ge(q_ready, 1)
                    for b in range(0, 8, 2):
                        nc.scalar.activation(full[:, BANK * b:BANK * b + 2 * BANK],
                                             full[:, BANK * b:BANK * b + 2 * BANK], ACT.Identity,
                                             bias=bq8[:, :], scale=0.125).then_inc(q_taken, 1)
                    act.wait_ge(norm_ready, 1)
                    nc.scalar.activation(st["struct"][:, :], st["struct"][:, :], ACT.Sqrt).then_inc(root, 1)

                @block.vector
                def _(dve):
                    v = nc.vector
                    do = Chain(dve, chain)
                    dve.wait_ge(vw_ready, 1)
                    v.tensor_tensor(moved[:, :, :], wide[:, :, 0:F], per_feature(bv), ALU.add).then_inc(vw_taken, 1)
                    dve.wait_ge(vw_taken, 2)
                    do(v.tensor_tensor(tmp[:, :, :], xw[:, :, :], xw[:, :, :], ALU.mult))
                    do(v.reduce_sum(st["struct"][:, :], tmp[:, :, :], AX.X))
                    v.tensor_scalar(st["struct"][:, :], st["struct"][:, :], NORM_FLOOR, None, ALU.max)\
                        .then_inc(norm_ready, 1)
                    do(v.tensor_tensor(tmp[:, :, :], cur[:, :, :], cur[:, :, :], ALU.mult))
                    do(v.reduce_sum(st["sumsq"][:, :], tmp[:, :, :], AX.X))
                    dve.wait_ge(q_taken, 4)
                    split(do, stationary=True, moving=False)

            accumulate(f"i{it}_edge", adj_b, column_sums=False)

            with phase(f"i{it}_edge_split") as (block, sem):
                acc_taken, twice_ready, chain = sem("acc_taken"), sem("twice_ready"), sem("dve_step")

                @block.tensor
                def _(pe):
                    pe.wait_ge(acc_taken, 1)
                    for b in range(8):
                        r = F * (b // 4)
                        for h in range(2):
                            last = nc.tensor.matmul(ps[F * h:F * h + F, b, :], ident[r:r + F, r:r + F],
                                                    accT[r:r + F, BANK * (b % 4):BANK * (b % 4) + BANK],
                                                    start=True, stop=True)
                    last.then_inc(twice_ready, 1)

                @block.vector
                def _(dve):
                    do = Chain(dve, chain)
                    nc.vector.tensor_copy(accT[:, :], fold4).then_inc(acc_taken, 1)
                    dve.wait_ge(twice_ready, 1)
                    split(do, stationary=False, moving=True)

            with phase(f"i{it}_attend") as (block, sem):
                loaded = [sem(f"block_loaded{s}") for s in range(SL3)]
                scores_ready, chunk_used, max_ready = sem("scores_ready"), sem("chunk_used"), sem("max_ready")
                seen = sem("scores_seen")
                exp_done, rz_ready, summed = sem("exp_done"), sem("rz_ready"), sem("summed")

                @block.sync
                def _(sp):
                    def body(t):
                        wait(sp, chunk_used, t.n * NC - (SL3 - 1) * NC)
                        sp.dma_start(held[t.slot(SL3)], adj_b[t.n]).then_inc(loaded[t.slot(SL3)], 16)
                    row_blocks(sp, 3, 5, 0, body)

                @block.tensor
                def _(pe):
                    for c in range(8):
                        g, j = c % 4, c // 4
                        nc.tensor.matmul(ps[32 * g:32 * g + 1, 6 + j, :], zeros_b[:, 0:1], zeros_b[:, :],
                                         start=True, stop=False, skip_group_check=True)

                    def column_sum(t):
                        s = t.slot(SL3)
                        pe.wait_ge(rz_ready, t.n + 1)
                        for c in range(8):
                            g, j = c % 4, c // 4
                            last = nc.tensor.matmul(ps[32 * g:32 * g + 1, 6 + j, :], rz[:, s:s + 1],
                                                    prod[s][:, BANK * c:BANK * c + BANK], start=False,
                                                    stop=False, skip_group_check=True)
                        last.then_inc(summed, 1)

                    def body(t):
                        score_products(pe, t, scores_ready, chunk_used)
                        if t.k >= 2:
                            column_sum(back(t, 2))
                    row_blocks(pe, 3, 5, 3, body)
                    for n in (NB - 2, NB - 1):
                        column_sum(Step(n, n, None, 3))

                @block.vector
                def _(dve):
                    def reciprocal(t):
                        s = t.slot(SL3)
                        dve.wait_ge(exp_done, t.n + 1)
                        nc.vector.reciprocal(rz[:, s:s + 1], zsum[:, s:s + 1]).then_inc(rz_ready, 1)

                    def body(t):
                        dve.wait_ge(loaded[t.slot(SL3)], 16 * (t.turn(SL3) + 1))
                        wait(dve, summed, t.n - 2)
                        weighted_scores(dve, t, seen, scores_ready, chunk_used, max_ready)
                        if t.k >= 1:
                            reciprocal(back(t, 1))
                    row_blocks(dve, 3, 5, 0, body)
                    reciprocal(Step(NB - 1, NB - 1, None, 3))

                @block.scalar
                def _(act):
                    row_blocks(act, 3, 5, 0, lambda t: exponentials(act, t, max_ready, exp_done))

            with phase(f"i{it}_component") as (block, sem):
                rows_taken, att_ready, chain = sem("rows_taken"), sem("att_ready"), sem("dve_step")
                norm_ready, root, xn_ready, twice_ready = (sem(n) for n in
                                                           ("norm_ready", "root", "xn_ready", "twice_ready"))
                sems = {n: sem(n) for n in SOFT}

                @block.scalar
                def _(act):
                    take_rows(act, 6, rows_taken)
                    global_softmax_scalar(act, sems)
                    act.wait_ge(norm_ready, 1)
                    nc.scalar.activation(st["feat"][:, :], st["feat"][:, :], ACT.Sqrt).then_inc(root, 1)

                @block.gpsimd
                def _(pool):
                    global_softmax_pool(pool, sems)

                @block.tensor
                def _(pe):
                    pe.wait_ge(rows_taken, 4)
                    rows_to_columns(0).then_inc(att_ready, 1)
                    pe.wait_ge(xn_ready, 1)
                    twice(tmp).then_inc(twice_ready, 1)

                @block.vector
                def _(dve):
                    v = nc.vector
                    do = Chain(dve, chain)
                    do(v.tensor_scalar(st["score"][:, :], st["struct"][:, :], 0.5, None, ALU.mult))
                    dve.wait_ge(att_ready, 1)
                    do(v.tensor_scalar(blocks4(st["mean"]), columns(0), 0.5 / N, None, ALU.mult))
                    do(v.tensor_tensor(st["score"][:, :], st["mean"][:, :], st["score"][:, :], ALU.add))
                    global_softmax_vector(dve, do, sems)
                    do(v.tensor_scalar(st["comp"][:, :], st["score"][:, :], th, None, ALU.is_ge))
                    do(v.tensor_scalar(st["refuse"][:, :], st["comp"][:, :], -REFUSE, REFUSE, ALU.mult, ALU.add))
                    do(v.tensor_tensor(st["feat"][:, :], st["sumsq"][:, :], st["comp"][:, :], ALU.mult))
                    v.tensor_scalar(st["feat"][:, :], st["feat"][:, :], NORM_FLOOR, None, ALU.max)\
                        .then_inc(norm_ready, 1)
                    dve.wait_ge(root, 1)
                    do(v.tensor_scalar(st["var"][:, :], st["feat"][:, :], 1e-8, None, ALU.max))
                    do(v.reciprocal(st["var"][:, :], st["var"][:, :]))
                    do(v.tensor_tensor(st["var"][:, :], st["var"][:, :], st["comp"][:, :], ALU.mult))
                    v.tensor_tensor(tmp[:, :, :], cur[:, :, :], per_node(st["var"]), ALU.mult).then_inc(xn_ready, 1)
                    dve.wait_ge(twice_ready, 1)
                    split(do, stationary=True, moving=True)

            with phase(f"i{it}_prune") as (block, sem):
                loaded = [sem(f"block_loaded{s}") for s in range(SL3)]
                stored = [sem(f"block_stored{s}") for s in range(SL3)]
                scores_ready, chunk_used, max_ready = sem("scores_ready"), sem("chunk_used"), sem("max_ready")
                seen = sem("scores_seen")
                exp_done, cut_ready, pruned = sem("exp_done"), sem("cut_ready"), sem("pruned")

                @block.sync
                def _(sp):
                    def store(t):
                        s = t.slot(SL3)
                        sp.wait_ge(pruned, t.n + 1)
                        sp.dma_start(Hp_b[t.n], prod[s]).then_inc(stored[s], 16)

                    def body(t):
                        if t.k >= SL3:
                            store(back(t, SL3))
                        sp.dma_start(held[t.slot(SL3)], adj_b[t.n]).then_inc(loaded[t.slot(SL3)], 16)
                    row_blocks(sp, 3, 5, 0, body)
                    for n in range(NB - SL3, NB):
                        store(Step(n, n, None, 3))
                    for s in range(SL3):
                        sp.wait_ge(stored[s], 16 * len(range(s, NB, SL3)))

                @block.tensor
                def _(pe):
                    row_blocks(pe, 3, 5, 0, lambda t: score_products(pe, t, scores_ready, chunk_used))

                @block.vector
                def _(dve):
                    def prune(t):
                        s = t.slot(SL3)
                        dve.wait_ge(exp_done, t.n + 1)
                        nc.vector.scalar_tensor_tensor(
                            out=cut[:, s:s + 1], in0=zsum[:, s:s + 1], scalar=th,
                            in1=st["refuse"][:, bass.ds(t.n, 1)], op0=ALU.mult, op1=ALU.add).then_inc(cut_ready, 1)
                        dve.wait_ge(cut_ready, t.n + 1)
                        nc.vector.scalar_tensor_tensor(
                            out=prod[s], in0=prod[s], scalar=cut[:, s:s + 1], in1=held[s],
                            op0=ALU.is_ge, op1=ALU.mult,
                            accum_out=st["conn"][:, bass.ds(t.n, 1)]).then_inc(pruned, 1)

                    def body(t):
                        s = t.slot(SL3)
                        dve.wait_ge(loaded[s], 16 * (t.turn(SL3) + 1))
                        wait(dve, stored[s], t.turn(SL3) * 16)
                        weighted_scores(dve, t, seen, scores_ready, chunk_used, max_ready)
                        if t.k >= 1:
                            prune(back(t, 1))
                    row_blocks(dve, 3, 5, 0, body)
                    prune(Step(NB - 1, NB - 1, None, 3))

                @block.scalar
                def _(act):
                    row_blocks(act, 3, 5, 0, lambda t: exponentials(act, t, max_ready, exp_done))

            with phase(f"i{it}_node") as (block, sem):
                chain, deg_floor, deg_root = sem("dve_step"), sem("deg_floor"), sem("deg_root")
                sems = {n: sem(n) for n in SOFT}

                @block.scalar
                def _(act):
                    global_softmax_scalar(act, sems)
                    act.wait_ge(deg_floor, 1)
                    nc.scalar.activation(st["dv"][:, :], st["dv"][:, :], ACT.Sqrt).then_inc(deg_root, 1)

                @block.gpsimd
                def _(pool):
                    global_softmax_pool(pool, sems)

                @block.vector
                def _(dve):
                    v = nc.vector
                    do = Chain(dve, chain)
                    v.tensor_scalar(st["dv"][:, :], st["conn"][:, :], DEG_EPS, None, ALU.max).then_inc(deg_floor, 1)
                    do(v.tensor_tensor(st["score"][:, :], st["conn"][:, :], st["feat"][:, :], ALU.mult))
                    global_softmax_vector(dve, do, sems)
                    do(v.scalar_tensor_tensor(out=st["node"][:, :], in0=st["score"][:, :], scalar=th,
                                              in1=st["comp"][:, :], op0=ALU.is_ge, op1=ALU.mult))
                    do(v.scalar_tensor_tensor(out=st["node"][:, :], in0=st["conn"][:, :], scalar=0.0,
                                              in1=st["node"][:, :], op0=ALU.is_gt, op1=ALU.mult))
                    dve.wait_ge(deg_root, 1)
                    do(v.reciprocal(st["dv"][:, :], st["dv"][:, :]))
                    do(v.tensor_tensor(st["node"][:, :], st["node"][:, :], st["dv"][:, :], ALU.mult))
                    do(v.tensor_tensor(moved[:, :, :], xw[:, :, :], per_node(st["node"]), ALU.mult))

            accumulate(f"i{it}_gather", Hp_b, column_sums=True)

            with phase(f"i{it}_gathered") as (block, sem):
                acc_taken, rows_taken, chain = sem("acc_taken"), sem("rows_taken"), sem("dve_step")
                nat_ready, deg_ready = sem("nat_ready"), sem("deg_ready")

                @block.scalar
                def _(act):
                    take_rows(act, 4, rows_taken)

                @block.tensor
                def _(pe):
                    pe.wait_ge(rows_taken, 4)
                    rows_to_columns(4).then_inc(deg_ready, 1)
                    pe.wait_ge(acc_taken, 1)
                    for b in range(NB):
                        h = b // HB
                        last = nc.tensor.matmul(nat4[:, b, :],
                                                accT[F * h:F * h + F, P * (b % HB):P * (b % HB) + P],
                                                ident[F * h:F * h + F, F * h:F * h + F], start=True, stop=True)
                    last.then_inc(nat_ready, 1)

                @block.vector
                def _(dve):
                    v = nc.vector
                    do = Chain(dve, chain)
                    v.tensor_copy(accT[:, :], fold4).then_inc(acc_taken, 1)
                    dve.wait_ge(deg_ready, 1)
                    do(v.tensor_scalar(blocks4(st["var"]), columns(4), DEG_EPS, None, ALU.max))
                    do(v.reciprocal(st["var"][:, :], st["var"][:, :]))
                    dve.wait_ge(nat_ready, 1)
                    do(v.tensor_tensor(moved[:, :, :], nat4, per_node(st["var"]), ALU.mult))

            with phase(f"i{it}_scatter") as (block, sem):
                SL = 4
                loaded = [sem(f"block_loaded{s}") for s in range(SL)]
                flipped = sem("chunk_flipped")
                taken = [sem("even_chunk_taken"), sem("odd_chunk_taken")]
                msg_ready, msg_taken, out_ready, out_taken = (sem(n) for n in
                                                              ("msg_ready", "msg_taken", "out_ready", "out_taken"))
                turned = [stream[:, 4 + s, :] for s in range(2)]

                @block.sync
                def _(sp):
                    def body(t):
                        wait(sp, flipped, t.n * NC - (SL - 1) * NC)
                        sp.dma_start(stream[:, t.slot(SL), :], Hp_b[t.n]).then_inc(loaded[t.slot(SL)], 16)
                    row_blocks(sp, 4, 4, 0, body)

                @block.tensor
                def _(pe):
                    def gather(t):
                        s = t.slot(2)
                        for q in range(2):
                            pe.wait_ge(taken[q], t.n * 2 + 2)
                        wait(pe, msg_taken, t.n - 1)
                        for jb in range(NB):
                            h = jb % 2
                            last = nc.tensor.matmul(ps[F * h:F * h + F, 4 + s, 0:P], moved[:, jb, :],
                                                    turned[s][:, P * jb:P * jb + P],
                                                    start=jb < 2, stop=jb >= NB - 2, skip_group_check=True)
                        last.then_inc(msg_ready, 1)

                    def finish(t):
                        s = t.slot(2)
                        pe.wait_ge(msg_taken, t.n + 1)
                        wait(pe, out_taken, t.n - 1)
                        nc.tensor.matmul(ps[:, 6 + s, 0:F], msgT[:, s, :], theta[:, :],
                                         start=True, stop=True).then_inc(out_ready, 1)

                    def body(t):
                        pe.wait_ge(loaded[t.slot(SL)], 16 * (t.turn(SL) + 1))
                        for q in range(NC):
                            wait(pe, taken[q % 2], t.n * 2 + q // 2)
                            for i in range(8):
                                jb = 8 * q + i
                                last = nc.tensor.transpose(ps[:, 2 * (q % 2) + i // 4, P * (i % 4):P * (i % 4) + P],
                                                           stream[:, t.slot(SL), P * jb:P * jb + P], ident[:, :])
                            last.then_inc(flipped, 1)
                        if t.k >= 1:
                            gather(back(t, 1))
                        if t.k >= 2:
                            finish(back(t, 2))
                    row_blocks(pe, 4, 4, 0, body)
                    gather(Step(NB - 1, NB - 1, None, 4))
                    finish(Step(NB - 2, NB - 2, None, 4))
                    finish(Step(NB - 1, NB - 1, None, 4))

                def take(e, copy, t, q):
                    e.wait_ge(flipped, t.n * NC + (q + 1))
                    wait(e, msg_ready, t.n - 1)
                    copy(turned[t.slot(2)][:, CHUNK * q:CHUNK * q + CHUNK],
                         ps[:, 2 * (q % 2):2 * (q % 2) + 2, :].rearrange("p a b -> p (a b)"))\
                        .then_inc(taken[q % 2], 1)

                @block.scalar
                def _(act):
                    def body(t):
                        for q in (0, 2):
                            take(act, nc.scalar.copy, t, q)
                    row_blocks(act, 4, 4, 0, body)

                @block.vector
                def _(dve):
                    def message(t):
                        s = t.slot(2)
                        dve.wait_ge(msg_ready, t.n + 1)
                        wait(dve, out_ready, t.n - 1)
                        nc.vector.tensor_copy(msgT[:, s, :], ps[:, 4 + s, 0:P]).then_inc(msg_taken, 1)

                    def output(t):
                        s = t.slot(2)
                        dve.wait_ge(out_ready, t.n + 1)
                        dst = cur[:, bass.ds(t.n, 1), :].rearrange("p a f -> p (a f)")
                        nc.vector.tensor_scalar(dst, ps[:, 6 + s, 0:F], st["dv"][:, bass.ds(t.n, 1)], 0.0,
                                                ALU.mult, ALU.max).then_inc(out_taken, 1)

                    def body(t):
                        for q in (1, 3):
                            take(dve, nc.vector.tensor_copy, t, q)
                        if t.k >= 2:
                            message(back(t, 2))
                        if t.k >= 3:
                            output(back(t, 3))
                    row_blocks(dve, 4, 4, 0, body)
                    for n in (NB - 2, NB - 1):
                        message(Step(n, n, None, 4))
                    for n in (NB - 3, NB - 2, NB - 1):
                        output(Step(n, n, None, 4))

            if not last_it:
                with phase(f"i{it}_fold") as (block, sem):
                    fold_ready, copied = sem("fold_ready"), sem("copied")

                    @block.tensor
                    def _(pe):
                        fold(cur).then_inc(fold_ready, 1)

                    @block.vector
                    def _(dve):
                        dve.wait_ge(fold_ready, 1)
                        nc.vector.tensor_copy(curT[:, :], fold4).then_inc(copied, 1)
                        dve.wait_ge(copied, 1)

        sup = [mov_a[:, 0:HALF], mov_a[:, HALF:N], mov_b[:, 0:HALF]]
        sup3 = sta_a[:, :]
        sup_all = streamb[:, 0:3 * HALF].rearrange("p (n t f) -> p n t f", t=3, f=F)
        with phase("support") as (block, sem):
            x_ready, fold_ready, fold_taken, sup_ready, chain = (
                sem(n) for n in ("x_ready", "fold_ready", "fold_taken", "sup_ready", "dve_step"))
            var_ready, std_ready = sem("var_ready"), sem("std_ready")

            @block.scalar
            def _(act):
                root_of_variance(act, var_ready, std_ready)

            @block.tensor
            def _(pe):
                pe.wait_ge(x_ready, 1)
                fold(res).then_inc(fold_ready, 1)
                pe.wait_ge(fold_taken, 1)
                project(nat4, curT, w3).then_inc(sup_ready, 1)

            @block.vector
            def _(dve):
                v = nc.vector
                do = Chain(dve, chain)
                do(v.tensor_tensor(res[:, :, :], res[:, :, :], cur[:, :, :], ALU.add))
                layer_norm(dve, do, res, res, var_ready, std_ready)
                v.tensor_copy(tmp[:, :, :], res[:, :, :]).then_inc(x_ready, 1)
                dve.wait_ge(fold_ready, 1)
                v.tensor_copy(curT[:, :], fold4).then_inc(fold_taken, 1)
                dve.wait_ge(sup_ready, 1)
                do(v.tensor_scalar(tmp[:, :, :], nat4, 2.0, None, ALU.mult))
                do(v.tensor_copy(sup_all[:, :, 0, :], tmp[:, :, :]))
                do(v.tensor_tensor(tmp[:, :, :], tmp[:, :, :], sup_all[:, :, 0, :], ALU.subtract))
                do(v.tensor_copy(sup_all[:, :, 1, :], tmp[:, :, :]))
                do(v.tensor_tensor(sup_all[:, :, 2, :], tmp[:, :, :], sup_all[:, :, 1, :], ALU.subtract))

        with phase("l3") as (block, sem):
            SL = 4
            loaded = [sem(f"block_loaded{s}") for s in range(SL)]
            masked, scanned, edges = sem("masked"), sem("scanned"), sem("edges_set")
            diff_ready, diff_taken, sum_ready, sum_taken = (sem(n) for n in
                                                            ("diff_ready", "diff_taken", "sum_ready", "sum_taken"))
            factor = [mov_a[:, :], mov_b[:, :]]
            decay = [streamb[:, 3 * HALF + (N + 2) * s:3 * HALF + (N + 2) * s + N + 1] for s in range(2)]
            weight = [mov_c[:, :], sta_a[:, :]]

            @block.sync
            def _(sp):
                def body(t):
                    wait(sp, masked, t.n - (SL - 1))
                    sp.dma_start(stream[:, t.slot(SL), :], adj_b[t.n]).then_inc(loaded[t.slot(SL)], 16)
                row_blocks(sp, 4, 4, 0, body)

            @block.vector
            def _(dve):
                v = nc.vector
                for s in range(2):
                    v.memset(decay[s][:, N:N + 1], 1.0).then_inc(edges, 1)

                def output(t):
                    dve.wait_ge(sum_ready, t.n + 1)
                    dst = cur[:, bass.ds(t.n, 1), :].rearrange("p a f -> p (a f)")
                    parts = ps[:, 6 + t.slot(2), 0:3 * F].rearrange("p (t f) -> p f t", t=3)
                    v.reduce_sum(dst, parts, AX.X).then_inc(sum_taken, 1)

                def body(t):
                    s = t.slot(2)
                    dve.wait_ge(loaded[t.slot(SL)], 16 * (t.turn(SL) + 1))
                    wait(dve, scanned, t.n - 1)
                    v.tensor_scalar(factor[s], stream[:, t.slot(SL), :], 0.0, 0.5, ALU.is_equal, ALU.max)\
                        .then_inc(masked, 1)
                    dve.wait_ge(masked, t.n + 1)
                    wait(dve, diff_ready, t.n * NC - NC)
                    v.tensor_tensor_scan(decay[s][:, N - 1::-1], factor[s][:, ::-1],
                                         floor_w[:, :].to_broadcast([P, N]), 1.0,
                                         ALU.mult, ALU.max).then_inc(scanned, 1)
                    if t.k >= 2:
                        output(back(t, 2))
                row_blocks(dve, 4, 4, 0, body)
                for n in (NB - 2, NB - 1):
                    output(Step(n, n, None, 4))

            @block.tensor
            def _(pe):
                pe.wait_ge(edges, 2)

                def combine(t):
                    s = t.slot(2)
                    pe.wait_ge(diff_taken, t.n * NC + NC)
                    wait(pe, sum_taken, t.n - 1)
                    for jb in range(NB):
                        last = nc.tensor.matmul(ps[:, 6 + s, 0:3 * F], weight[s][:, P * jb:P * jb + P],
                                                sup_all[:, jb, :, :].rearrange("p t f -> p (t f)"),
                                                start=jb == 0, stop=jb == NB - 1)
                    last.then_inc(sum_ready, 1)

                def body(t):
                    s = t.slot(2)
                    pe.wait_ge(scanned, t.n + 1)
                    for q in range(NC):
                        wait(pe, diff_taken, t.n * NC + (q - 1))
                        for i in range(8):
                            jb = 8 * q + i
                            out = ps[:, 2 * (q % 2) + i // 4, P * (i % 4):P * (i % 4) + P]
                            nc.tensor.matmul(out, decay[s][:, P * jb + 1:P * jb + 1 + P], ident_b[:, :],
                                             start=True, stop=False)
                            last = nc.tensor.matmul(out, decay[s][:, P * jb:P * jb + P], neg_ident_b[:, :],
                                                    start=False, stop=True)
                        last.then_inc(diff_ready, 1)
                    if t.k >= 1:
                        combine(back(t, 1))
                row_blocks(pe, 4, 4, 0, body)
                combine(Step(NB - 1, NB - 1, None, 4))

            @block.scalar
            def _(act):
                def body(t):
                    for q in range(NC):
                        act.wait_ge(diff_ready, t.n * NC + (q + 1))
                        wait(act, sum_ready, t.n - 1)
                        nc.scalar.copy(weight[t.slot(2)][:, CHUNK * q:CHUNK * q + CHUNK],
                                       ps[:, 2 * (q % 2):2 * (q % 2) + 2, :].rearrange("p a b -> p (a b)"))\
                            .then_inc(diff_taken, 1)
                row_blocks(act, 4, 4, 0, body)

        with phase("out") as (block, sem):
            chain, out_stored, out_made = sem("dve_step"), sem("out_stored"), sem("out_made")
            var_ready, std_ready = sem("var_ready"), sem("std_ready")

            @block.scalar
            def _(act):
                root_of_variance(act, var_ready, std_ready)

            @block.vector
            def _(dve):
                v = nc.vector
                do = Chain(dve, chain)
                do(v.tensor_tensor(cur[:, :, :], cur[:, :, :], per_feature(b3), ALU.add))
                do(v.tensor_tensor(cur[:, :, :], cur[:, :, :], res[:, :, :], ALU.add))
                layer_norm(dve, do, cur, cur, var_ready, std_ready)
                v.tensor_copy(res[:, :, :], cur[:, :, :]).then_inc(out_made, 1)

            @block.sync
            def _(sp):
                sp.wait_ge(out_made, 1)
                sp.dma_start(d["out"].rearrange("(n p) f -> p n f", p=P), res[:, :, :]).then_inc(out_stored, 16)
                sp.wait_ge(out_stored, 16)


def kernel(**inputs):
    import numpy as np
    import concourse.bacc as bacc
    from concourse.bass_utils import run_bass_kernel_spmd as run

    nc = bacc.Bacc("TRN2", target_bir_lowering=False, num_devices=1)
    adj = np.asarray(inputs["adj"])
    x = np.asarray(inputs["x"])
    arrays = {
        "x": x, "xT": x.T, "adj": adj, "adjT": adj.T,
        "W0": inputs["L0_gnn_W"], "b0": inputs["L0_gnn_b"], "W1T": np.asarray(inputs["L1_gnn_W"]).T,
        "W": inputs["L2_gnn_W"], "Theta": inputs["L2_gnn_Theta"], "Wq": inputs["L2_gnn_Wq"],
        "bq": inputs["L2_gnn_bq"], "Wv": inputs["L2_gnn_Wv"], "bv": inputs["L2_gnn_bv"],
        "W3": inputs["L3_gnn_weight"], "b3": inputs["L3_gnn_bias"],
    }
    arrays = {n: np.ascontiguousarray(a) for n, a in arrays.items()}
    d = {n: nc.dram_tensor(f"in_{n}", a.shape, F32, kind="ExternalInput").ap() for n, a in arrays.items()}
    d["out"] = nc.dram_tensor("out", (N, F), F32, kind="ExternalOutput").ap()
    build(nc, d)
    r = run(nc, [{f"in_{n}": a for n, a in arrays.items()}], core_ids=[0])
    return r.results[0]["out"]
```

```python
import concourse.bass as bass
from concourse import mybir
from contextlib import ExitStack, contextmanager
import numpy as np

F32 = mybir.dt.float32
BF16 = mybir.dt.bfloat16
ALU = mybir.AluOpType
ACT = mybir.ActivationFunctionType
AX = mybir.AxisListType

P = 128
N = 4096
F = 64
NB = N // P
HALF = N // 2
HB = NB // 2
BANK = 512
LN_EPS = 1e-5
DEG_EPS = 1e-6
NORM_FLOOR = 1e-16
NEG_HUGE = -3.0e38
REFUSE = 1.0e30
W_FLOOR = 2.0 ** -100
THETAS = [0.000244 + (1.0 - float(np.exp(-0.1 * it))) * (0.0003 - 0.000244) for it in range(2)]


class Step:

    def __init__(self, n, k, it, unroll):
        self.n, self.k, self.it, self.unroll = n, k, it, unroll

    def slot(self, slots):
        return self.k % slots

    def turn(self, slots):
        if self.it is None:
            return self.k // slots
        assert self.unroll % slots == 0
        return self.it * (self.unroll // slots) + self.k // slots


def row_blocks(e, unroll, lead, tail, body):
    groups = (NB - lead - tail) // unroll
    assert lead + tail + groups * unroll == NB
    for n in range(lead):
        body(Step(n, n, None, unroll))
    with e.Fori(0, groups) as it:
        for u in range(unroll):
            body(Step(it * unroll + (lead + u), lead + u, it, unroll))
    for n in range(NB - tail, NB):
        body(Step(n, n, None, unroll))


def wait(e, sem, value):
    if isinstance(value, int) and value <= 0:
        return
    e.wait_ge(sem, value)


def build(nc, d):
    ctx = ExitStack()
    with ctx:
        def sb(name, shape, dt=F32):
            return ctx.enter_context(nc.sbuf_tensor(name, shape, dt))

        ps = ctx.enter_context(nc.psum_tensor("ps", [P, 8, BANK], F32))
        res = sb("res", [P, NB, F])
        cur = sb("cur", [P, NB, F])
        moved = sb("moved", [P, NB, F])
        xw = sb("xw", [P, NB, F])
        tmp = sb("tmp", [P, NB, F])
        accT = sb("accT", [P, HALF])
        curT = sb("curT", [P, HALF])
        rows = sb("rows", [P, 2 * BANK])
        mov_a = sb("mov_a", [P, N], BF16)
        mov_b = sb("mov_b", [P, N], BF16)
        mov_c = sb("mov_c", [P, N], BF16)
        sta_a = sb("sta_a", [P, N], BF16)
        sta_b = sb("sta_b", [P, N], BF16)
        stage = sb("stage", [P, 4, F])
        ident = sb("ident", [P, P])
        ident_b = sb("ident_b", [P, P], BF16)
        neg_ident_b = sb("neg_ident_b", [P, P], BF16)
        ones = sb("ones", [P, 1])
        zeros_b = sb("zeros_b", [P, BANK], BF16)
        floor_w = sb("floor_w", [P, 1])
        w0, w1s, w1n, wq, wv, w2, theta, w3 = (
            sb(n, [P, F]) for n in ("w0", "w1s", "w1n", "wq", "wv", "w2", "theta", "w3"))
        b0, bv, b3 = (sb(n, [P, F]) for n in ("b0", "bv", "b3"))
        bq8 = sb("bq8", [P, 1])
        st = {n: sb(n, [P, NB]) for n in ("mean", "var", "std", "rdeg", "struct", "sumsq", "comp", "feat",
                                          "refuse", "conn", "dv", "score", "node")}
        gl = {n: sb(n, [P, 1]) for n in ("gmax", "gmaxall", "gneg", "gsum", "gsumall", "grec")}
        mx4 = sb("mx4", [P, 3, 4])
        negmax = sb("negmax", [P, 3])
        zsum = sb("zsum", [P, 3])
        rz = sb("rz", [P, 3])
        cut = sb("cut", [P, 3])
        msgT = sb("msgT", [P, 2, P])
        stream = sb("stream", [P, 6, N])
        streamb = stream[:, 4:6, :].rearrange("p s n -> p (s n)").bitcast(BF16)

        Hp = nc.dram_tensor("pruned", (NB, 4, P, N // 4), F32, kind="Internal").ap()
        Hp_rows = Hp.rearrange("n q p j -> n p q j")
        Hp_quarters = Hp.rearrange("n q (r g) j -> n (q r) (g j)", g=4)

        def by_rows(m):
            return m.rearrange("(n p) c -> n p c", p=P)

        adj_b, adjT_b = by_rows(d["adj"]), by_rows(d["adjT"])

        def quarters(a):
            return a.rearrange("p (q j) -> p q j", q=4)

        @contextmanager
        def phase(name):
            made = []

            def sem(n):
                s = nc.alloc_semaphore(f"{name}_{n}")
                made.append(s)
                return s

            with nc.Block() as block:
                yield block, sem
            nc.clear_and_free_semaphores(made)
            nc.all_engine_barrier()

        nat4 = ps[:, 0:4, :].rearrange("p b (k f) -> p (b k) f", f=F)
        nat4b = ps[:, 4:8, :].rearrange("p b (k f) -> p (b k) f", f=F)
        fold4 = ps[:, 0:4, :].rearrange("p b c -> p (b c)")
        fold4b = ps[:, 4:8, :].rearrange("p b c -> p (b c)")

        def per_node(a):
            return a[:, :].unsqueeze(2).to_broadcast([P, NB, F])

        def per_feature(a):
            return a[:, :].unsqueeze(1).to_broadcast([P, NB, F])

        def project(dst, srcT, w):
            for b in range(NB):
                r = F * (b // HB)
                c = P * (b % HB)
                last = nc.tensor.matmul(dst[:, b, :], srcT[r:r + F, c:c + P], w[r:r + F, :], start=True, stop=True)
            return last

        def fold(src, dst):
            for c in range(HB):
                for h in range(2):
                    last = nc.tensor.matmul(dst[F * h:F * h + F, P * c:P * c + P], src[:, HB * h + c, :],
                                            ident[:, :], start=True, stop=True)
            return last

        def rows_to_columns(bank):
            for b in range(NB):
                chunk, off = divmod(P * b, BANK)
                g, j = chunk % 4, chunk // 4
                at = 4 * j + b % 4
                last = nc.tensor.matmul(ps[:, bank + g, at:at + 1],
                                        rows[32 * g:32 * g + 1, BANK * j + off:BANK * j + off + P],
                                        ones[32 * g:32 * g + 1, :], start=True, stop=True)
            return last

        def columns(bank):
            return ps[:, bank:bank + 4, 0:8].rearrange("p g (j i) -> p j g i", i=4)

        def blocks4(a):
            return a[:, :].rearrange("p (j g i) -> p j g i", j=2, g=4)

        class Chain:

            def __init__(self, e, sem):
                self.e, self.sem, self.count = e, sem, 0

            def __call__(self, ins):
                self.count += 1
                ins.then_inc(self.sem, 1)
                self.e.wait_ge(self.sem, self.count)

        def layer_norm(dve, do, dst, y, var_ready, std_ready):
            v = nc.vector
            do(v.reduce_sum(st["mean"][:, :], y[:, :, :], AX.X))
            do(v.tensor_scalar(st["mean"][:, :], st["mean"][:, :], 1.0 / F, None, ALU.mult))
            do(v.tensor_tensor(y[:, :, :], y[:, :, :], per_node(st["mean"]), ALU.subtract))
            do(v.tensor_tensor(tmp[:, :, :], y[:, :, :], y[:, :, :], ALU.mult))
            do(v.reduce_sum(st["var"][:, :], tmp[:, :, :], AX.X))
            v.tensor_scalar(st["var"][:, :], st["var"][:, :], 1.0 / F, LN_EPS, ALU.mult, ALU.add)\
                .then_inc(var_ready, 1)
            dve.wait_ge(std_ready, 1)
            do(v.reciprocal(st["std"][:, :], st["std"][:, :]))
            do(v.tensor_tensor(dst[:, :, :], y[:, :, :], per_node(st["std"]), ALU.mult))

        def root_of_variance(act, var_ready, std_ready):
            act.wait_ge(var_ready, 1)
            nc.scalar.activation(st["std"][:, :], st["var"][:, :], ACT.Sqrt).then_inc(std_ready, 1)

        TOP, LOW = slice(0, F), slice(F, P)
        rest = stream[:, 5, HALF:N]
        hi, mid, lo = (streamb[:, N + HALF * i:N + HALF * i + HALF] for i in range(3))

        def split(do, src):
            v = nc.vector
            do(v.tensor_copy(hi, src))
            do(v.tensor_tensor(rest, src, hi, ALU.subtract))
            do(v.tensor_copy(mid, rest))
            do(v.tensor_tensor(lo, rest, mid, ALU.subtract))

        def spread(copy, dst, top, low):
            for part, rows_out in ((top, TOP), (low, LOW)):
                for h in range(2):
                    last = copy(dst[rows_out, HALF * h:HALF * h + HALF], part[F * h:F * h + F, :])
            return last

        def accumulate(block, sem, matrix_b, column_sums, moved_ready, banks_free, side=None):
            SL = 4
            loaded = [sem(f"block_loaded{s}") for s in range(SL)]
            staged = sem("stationary_staged")
            used = sem("block_used")

            @block.sync
            def _(sp):
                def body(t):
                    wait(sp, used, t.n - (SL - 1))
                    dst = stream[:, t.slot(SL), :]
                    if matrix_b is Hp_rows:
                        dst = quarters(dst)
                    sp.dma_start(dst, matrix_b[t.n]).then_inc(loaded[t.slot(SL)], 16)
                row_blocks(sp, SL, SL, 0, body)

            @block.scalar
            def _(act):
                act.wait_ge(*moved_ready)

                def body(t):
                    wait(act, used, t.n - (SL - 1))
                    src = moved[:, t.n, :] if isinstance(t.n, int) else \
                        moved[:, bass.ds(t.n, 1), :].rearrange("p a f -> p (a f)")
                    nc.scalar.activation(stage[:, t.slot(SL), :], src, ACT.Copy).then_inc(staged, 1)
                row_blocks(act, SL, SL, 0, body)

            @block.tensor
            def _(pe):
                pe.wait_ge(*banks_free)
                for b in range(4):
                    for h in range(2):
                        nc.tensor.matmul(ps[F * h:F * h + F, b, :], zeros_b[:, 0:F], zeros_b[:, :],
                                         start=True, stop=False, skip_group_check=True)
                if column_sums:
                    for c in range(8):
                        g, j = c % 4, c // 4
                        nc.tensor.matmul(ps[32 * g:32 * g + 1, 4 + j, :], zeros_b[:, 0:1], zeros_b[:, :],
                                         start=True, stop=False, skip_group_check=True)

                def body(t):
                    s = t.slot(SL)
                    pe.wait_ge(loaded[s], 16 * (t.turn(SL) + 1))
                    pe.wait_ge(staged, t.n + 1)
                    for b in range(4):
                        for h in range(2):
                            c = HALF * h + BANK * b
                            last = nc.tensor.matmul(ps[F * h:F * h + F, b, :], stage[:, s, :],
                                                    stream[:, s, c:c + BANK], start=False, stop=False,
                                                    skip_group_check=True)
                    if column_sums:
                        for c in range(8):
                            g, j = c % 4, c // 4
                            last = nc.tensor.matmul(ps[32 * g:32 * g + 1, 4 + j, :], ones[:, :],
                                                    stream[:, s, BANK * c:BANK * c + BANK], start=False,
                                                    stop=False, skip_group_check=True)
                    last.then_inc(used, 1)
                    if t.it is None and t.k == SL - 1 and side:
                        side(pe)
                row_blocks(pe, SL, SL, 0, body)

        def edge_pass(block, sem, cur_ready):
            fold_ready, fold_taken, v_ready, v_taken = (sem(n) for n in
                                                        ("cur_folded", "cur_taken", "v_ready", "v_taken"))
            xw_ready, xw_taken, q_ready, q_taken = (sem(n) for n in ("xw_ready", "xw_taken", "q_ready", "q_taken"))
            norm_ready, root, chain = sem("norm_ready"), sem("root"), sem("edge_step")

            @block.tensor
            def _(pe):
                pe.wait_ge(*cur_ready)
                fold(cur, fold4).then_inc(fold_ready, 1)
                pe.wait_ge(fold_taken, 1)
                project(nat4b, curT, wv).then_inc(v_ready, 1)

            @block.vector
            def _(dve):
                v = nc.vector
                do = Chain(dve, chain)
                dve.wait_ge(fold_ready, 1)
                v.tensor_copy(curT[:, :], fold4).then_inc(fold_taken, 1)
                dve.wait_ge(v_ready, 1)
                v.tensor_tensor(moved[:, :, :], nat4b, per_feature(bv), ALU.add).then_inc(v_taken, 1)
                dve.wait_ge(xw_ready, 1)
                v.tensor_copy(xw[:, :, :], nat4b).then_inc(xw_taken, 1)
                dve.wait_ge(q_ready, 1)
                v.tensor_scalar(accT[:, :], fold4b, 0.125, bq8[:, :], ALU.mult, ALU.add).then_inc(q_taken, 1)
                dve.wait_ge(q_taken, 1)
                split(do, accT[:, :])
                do(spread(v.tensor_copy, sta_a, hi, mid))
                do(spread(v.tensor_copy, sta_b, hi, lo))
                do(v.tensor_tensor(tmp[:, :, :], xw[:, :, :], xw[:, :, :], ALU.mult))
                do(v.reduce_sum(st["struct"][:, :], tmp[:, :, :], AX.X))
                do(v.tensor_scalar(st["struct"][:, :], st["struct"][:, :], NORM_FLOOR, None, ALU.max))
                do(v.tensor_tensor(tmp[:, :, :], cur[:, :, :], cur[:, :, :], ALU.mult))
                do(v.reduce_sum(st["sumsq"][:, :], tmp[:, :, :], AX.X))

            def side(pe):
                pe.wait_ge(v_taken, 1)
                project(nat4b, curT, w2).then_inc(xw_ready, 1)
                pe.wait_ge(xw_taken, 1)
                for b in range(4):
                    for h in range(2):
                        r = slice(F * h, F * h + F)
                        last = nc.tensor.matmul(ps[r, 4 + b, :], wq[r, :], curT[r, BANK * b:BANK * b + BANK],
                                                start=True, stop=True)
                last.then_inc(q_ready, 1)

            accumulate(block, sem, adj_b, False, (v_taken, 1), (fold_taken, 1), side)

        def take_rows(act, base, taken):
            for g in range(4):
                nc.scalar.activation(rows[32 * g:32 * g + 1, :],
                                     ps[32 * g:32 * g + 1, base:base + 2, :].rearrange("p a b -> p (a b)"),
                                     ACT.Copy).then_inc(taken, 1)

        with phase("l0") as (block, sem):
            small_loaded, ident_zero, ident_made = sem("small_loaded"), sem("ident_zero"), sem("ident_made")
            h_ready, h_taken, chain = sem("h_ready"), sem("h_taken"), sem("dve_step")
            loads = [(res[:, :, :], d["x"].rearrange("(n p) f -> p n f", p=P))]
            for h in range(2):
                r = slice(F * h, F * h + F)
                loads += [(curT[r, :], d["xT"][:, HALF * h:HALF * h + HALF]),
                          (w0[r, :], d["W0"]), (w1s[r, :], d["W1T"][0:F, :]), (w1n[r, :], d["W1T"][F:P, :]),
                          (wq[r, :], d["Wq"]), (wv[r, :], d["Wv"]), (w2[r, :], d["W"]), (theta[r, :], d["Theta"]), (w3[r, :], d["W3"]),
                          (bq8[r, :], d["bq"].rearrange("(f a) -> f a", a=1))]
            for t, n in ((b0, "b0"), (bv, "bv"), (b3, "b3")):
                loads += [(t[:, :], d[n].rearrange("(a f) -> a f", a=1).broadcast_to([P, F]))]

            @block.sync
            def _(sp):
                for dst, src in loads:
                    sp.dma_start(dst, src).then_inc(small_loaded, 16)

            @block.gpsimd
            def _(pool):
                nc.gpsimd.memset(ident[:, :], 0.0).then_inc(ident_zero, 1)
                pool.wait_ge(ident_zero, 1)
                nc.gpsimd.affine_select(out=ident[:, :], in_=ident[:, :], compare_op=ALU.not_equal, fill=1.0,
                                        base=0, pattern=[[-1, P]], channel_multiplier=1).then_inc(ident_made, 1)

            @block.tensor
            def _(pe):
                pe.wait_ge(small_loaded, 16 * len(loads))
                project(nat4, curT, w0).then_inc(h_ready, 1)

            @block.vector
            def _(dve):
                v = nc.vector
                do = Chain(dve, chain)
                do(v.memset(ones[:, :], 1.0))
                do(v.memset(zeros_b[:, :], 0.0))
                do(v.memset(floor_w[:, :], W_FLOOR))
                dve.wait_ge(ident_made, 1)
                do(v.tensor_copy(ident_b[:, :], ident[:, :]))
                do(v.tensor_scalar(neg_ident_b[:, :], ident[:, :], -1.0, None, ALU.mult))
                dve.wait_ge(small_loaded, 16 * len(loads))
                do(v.tensor_scalar(bq8[:, :], bq8[:, :], 0.125, None, ALU.mult))
                dve.wait_ge(h_ready, 1)
                v.tensor_copy(moved[:, :, :], nat4).then_inc(h_taken, 1)

            accumulate(block, sem, adjT_b, True, (h_taken, 1), (h_taken, 1))

        with phase("l1") as (block, sem):
            acc_taken, rows_taken, chain = sem("acc_taken"), sem("rows_taken"), sem("dve_step")
            nat_ready, deg_ready, x_ready, fold_ready = (sem(n) for n in
                                                         ("nat_ready", "deg_ready", "x_ready", "fold_ready"))
            deg_taken, fold_taken, self_ready = sem("deg_taken"), sem("fold_taken"), sem("self_ready")
            var_ready, std_ready = sem("var_ready"), sem("std_ready")

            @block.scalar
            def _(act):
                take_rows(act, 4, rows_taken)
                root_of_variance(act, var_ready, std_ready)

            @block.tensor
            def _(pe):
                pe.wait_ge(rows_taken, 4)
                rows_to_columns(4).then_inc(deg_ready, 1)
                pe.wait_ge(acc_taken, 1)
                for b in range(NB):
                    h = b // HB
                    last = nc.tensor.matmul(nat4[:, b, :], accT[F * h:F * h + F, P * (b % HB):P * (b % HB) + P],
                                            ident[F * h:F * h + F, F * h:F * h + F], start=True, stop=True)
                last.then_inc(nat_ready, 1)

            @block.vector
            def _(dve):
                v = nc.vector
                do = Chain(dve, chain)
                v.tensor_copy(accT[:, :], fold4).then_inc(acc_taken, 1)
                do(v.tensor_tensor(res[:, :, :], res[:, :, :], per_feature(b0), ALU.add))
                dve.wait_ge(nat_ready, 1)
                do(v.tensor_tensor(res[:, :, :], nat4, res[:, :, :], ALU.add))
                layer_norm(dve, do, res, res, var_ready, std_ready)
                v.tensor_copy(moved[:, :, :], res[:, :, :]).then_inc(x_ready, 1)
                dve.wait_ge(deg_ready, 1)
                v.tensor_scalar(blocks4(st["rdeg"]), columns(4), 1.0, None, ALU.max).then_inc(deg_taken, 1)
                dve.wait_ge(deg_taken, 1)
                do(v.reciprocal(st["rdeg"][:, :], st["rdeg"][:, :]))
                dve.wait_ge(fold_ready, 1)
                v.tensor_copy(curT[:, :], fold4b).then_inc(fold_taken, 1)
                dve.wait_ge(self_ready, 1)
                do(v.tensor_copy(cur[:, :, :], nat4b))

            def side(pe):
                pe.wait_ge(deg_taken, 1)
                fold(res, fold4b).then_inc(fold_ready, 1)
                pe.wait_ge(fold_taken, 1)
                project(nat4b, curT, w1s).then_inc(self_ready, 1)

            accumulate(block, sem, adjT_b, False, (x_ready, 1), (x_ready, 1), side)

        with phase("i0_edge") as (block, sem):
            acc_taken, chain, x_ready, nb_ready = (sem(n) for n in
                                                   ("acc_taken", "dve_step", "x_ready", "neighbours_ready"))
            var_ready, std_ready = sem("var_ready"), sem("std_ready")

            @block.scalar
            def _(act):
                root_of_variance(act, var_ready, std_ready)

            @block.tensor
            def _(pe):
                pe.wait_ge(acc_taken, 1)
                project(nat4, accT, w1n).then_inc(nb_ready, 1)

            @block.vector
            def _(dve):
                v = nc.vector
                do = Chain(dve, chain)
                v.tensor_copy(accT[:, :], fold4).then_inc(acc_taken, 1)
                dve.wait_ge(nb_ready, 1)
                do(v.tensor_tensor(tmp[:, :, :], nat4, per_node(st["rdeg"]), ALU.mult))
                do(v.tensor_tensor(cur[:, :, :], tmp[:, :, :], cur[:, :, :], ALU.add))
                do(v.scalar_tensor_tensor(out=res[:, :, :].rearrange("p n f -> p (n f)"),
                                          in0=cur[:, :, :].rearrange("p n f -> p (n f)"), scalar=0.0,
                                          in1=res[:, :, :].rearrange("p n f -> p (n f)"),
                                          op0=ALU.max, op1=ALU.add))
                layer_norm(dve, do, res, res, var_ready, std_ready)
                v.tensor_copy(cur[:, :, :], res[:, :, :]).then_inc(x_ready, 1)

            edge_pass(block, sem, (x_ready, 1))

        def global_softmax_vector(dve, do, sems):
            v = nc.vector
            v.reduce_max(gl["gmax"][:, :], st["score"][:, :], AX.X).then_inc(sems["part_max"], 1)
            dve.wait_ge(sems["all_max"], 1)
            v.tensor_scalar(gl["gneg"][:, :], gl["gmaxall"][:, :], -1.0, None, ALU.mult)\
                .then_inc(sems["bias_ready"], 1)
            dve.wait_ge(sems["all_sum"], 1)
            do(v.reciprocal(gl["grec"][:, :], gl["gsumall"][:, :]))
            do(v.tensor_scalar(st["score"][:, :], st["score"][:, :], gl["grec"][:, :], None, ALU.mult))

        def global_softmax_pool(pool, sems):
            pool.wait_ge(sems["part_max"], 1)
            nc.gpsimd.partition_all_reduce(gl["gmaxall"][:, :], gl["gmax"][:, :], P,
                                           bass.bass_isa.ReduceOp.max).then_inc(sems["all_max"], 1)
            pool.wait_ge(sems["part_sum"], 1)
            nc.gpsimd.partition_all_reduce(gl["gsumall"][:, :], gl["gsum"][:, :], P,
                                           bass.bass_isa.ReduceOp.add).then_inc(sems["all_sum"], 1)

        def global_softmax_scalar(act, sems):
            act.wait_ge(sems["bias_ready"], 1)
            nc.scalar.activation(st["score"][:, :], st["score"][:, :], ACT.Exp, bias=gl["gneg"][:, :],
                                 accum_out=gl["gsum"][:, :]).then_inc(sems["part_sum"], 1)

        SOFT = ("part_max", "all_max", "bias_ready", "part_sum", "all_sum")
        SL3 = 3
        CHUNK = 2 * BANK
        NC = N // CHUNK
        held = [stream[:, s, :] for s in range(3)]
        prod = [stream[:, 3 + s, :] for s in range(3)]

        def score_products(pe, t, scores_ready, chunk_used):
            for c in range(NC):
                slot = (NC * t.k + c) % SL3
                wait(pe, chunk_used, t.n * NC + (c - 2))
                for j in range(2):
                    cols = slice(CHUNK * c + BANK * j, CHUNK * c + BANK * j + BANK)
                    rows_n = bass.ds(t.n * P, P)
                    out = ps[:, 2 * slot + j, :]
                    nc.tensor.matmul(out, sta_a[:, rows_n], mov_a[:, cols], start=True, stop=False)
                    nc.tensor.matmul(out, sta_a[:, rows_n], mov_b[:, cols], start=False, stop=False)
                    last = nc.tensor.matmul(out, sta_b[:, rows_n], mov_c[:, cols], start=False, stop=True)
                last.then_inc(scores_ready, 1)

        def weighted_scores(dve, t, seen, scores_ready, chunk_used, max_ready):
            s = t.slot(SL3)
            for c in range(NC):
                slot = (NC * t.k + c) % SL3
                dve.wait_ge(scores_ready, t.n * NC + (c + 1))
                dve.sem_inc(seen, 1)
                cols = slice(CHUNK * c, CHUNK * c + CHUNK)
                nc.vector.tensor_tensor_reduce(
                    out=prod[s][:, cols], in0=ps[:, 2 * slot:2 * slot + 2, :].rearrange("p a b -> p (a b)"),
                    in1=held[s][:, cols], scale=1.0, scalar=NEG_HUGE, op0=ALU.mult, op1=ALU.max,
                    accum_out=mx4[:, s, c:c + 1]).then_inc(chunk_used, 1)
            dve.wait_ge(chunk_used, t.n * NC + NC)
            nc.vector.tensor_reduce(negmax[:, s:s + 1], mx4[:, s, :], AX.X, ALU.max, negate=True)\
                .then_inc(max_ready, 1)

        def exponentials(act, t, max_ready, exp_done):
            s = t.slot(SL3)
            act.wait_ge(max_ready, t.n + 1)
            nc.scalar.activation(prod[s], prod[s], ACT.Exp, bias=negmax[:, s:s + 1],
                                 accum_out=zsum[:, s:s + 1]).then_inc(exp_done, 1)

        def back(t, by):
            return Step(t.n - by, t.k - by, t.it, t.unroll)

        for it in range(2):
            th = THETAS[it]
            last_it = it == 1

            with phase(f"i{it}_attend") as (block, sem):
                loaded = [sem(f"block_loaded{s}") for s in range(SL3)]
                scores_ready, chunk_used, max_ready = sem("scores_ready"), sem("chunk_used"), sem("max_ready")
                seen = sem("scores_seen")
                exp_done, rz_ready, summed = sem("exp_done"), sem("rz_ready"), sem("summed")
                spread_done, banks_read, chain, root = (sem(n) for n in
                                                        ("spread_done", "banks_read", "dve_step", "root"))

                @block.scalar
                def _(act):
                    nc.scalar.activation(st["struct"][:, :], st["struct"][:, :], ACT.Sqrt).then_inc(root, 1)
                    act.wait_ge(root, 1)

                @block.vector
                def _(dve):
                    v = nc.vector
                    do = Chain(dve, chain)
                    v.tensor_copy(accT[:, :], fold4).then_inc(banks_read, 1)
                    dve.wait_ge(banks_read, 1)
                    split(do, accT[:, :])
                    spread(v.tensor_copy, mov_a, hi, hi).then_inc(spread_done, 1)
                    spread(v.tensor_copy, mov_b, mid, mid).then_inc(spread_done, 1)
                    spread(v.tensor_copy, mov_c, lo, hi).then_inc(spread_done, 1)
                    dve.wait_ge(spread_done, 3)

                @block.sync
                def _(sp):
                    def body(t):
                        wait(sp, chunk_used, t.n * NC - (SL3 - 1) * NC)
                        sp.dma_start(held[t.slot(SL3)], adj_b[t.n]).then_inc(loaded[t.slot(SL3)], 16)
                    row_blocks(sp, 3, 5, 0, body)

                @block.tensor
                def _(pe):
                    pe.wait_ge(banks_read, 1)
                    pe.wait_ge(spread_done, 3)
                    for c in range(8):
                        g, j = c % 4, c // 4
                        nc.tensor.matmul(ps[32 * g:32 * g + 1, 6 + j, :], zeros_b[:, 0:1], zeros_b[:, :],
                                         start=True, stop=False, skip_group_check=True)

                    def column_sum(t):
                        s = t.slot(SL3)
                        pe.wait_ge(rz_ready, t.n + 1)
                        for c in range(8):
                            g, j = c % 4, c // 4
                            last = nc.tensor.matmul(ps[32 * g:32 * g + 1, 6 + j, :], rz[:, s:s + 1],
                                                    prod[s][:, BANK * c:BANK * c + BANK], start=False,
                                                    stop=False, skip_group_check=True)
                        last.then_inc(summed, 1)

                    def body(t):
                        score_products(pe, t, scores_ready, chunk_used)
                        if t.k >= 2:
                            column_sum(back(t, 2))
                    row_blocks(pe, 3, 5, 3, body)
                    for n in (NB - 2, NB - 1):
                        column_sum(Step(n, n, None, 3))

                @block.vector
                def _(dve):
                    def reciprocal(t):
                        s = t.slot(SL3)
                        dve.wait_ge(exp_done, t.n + 1)
                        nc.vector.reciprocal(rz[:, s:s + 1], zsum[:, s:s + 1]).then_inc(rz_ready, 1)

                    def body(t):
                        dve.wait_ge(loaded[t.slot(SL3)], 16 * (t.turn(SL3) + 1))
                        wait(dve, summed, t.n - 2)
                        weighted_scores(dve, t, seen, scores_ready, chunk_used, max_ready)
                        if t.k >= 1:
                            reciprocal(back(t, 1))
                    row_blocks(dve, 3, 5, 0, body)
                    reciprocal(Step(NB - 1, NB - 1, None, 3))

                @block.scalar
                def _(act):
                    row_blocks(act, 3, 5, 0, lambda t: exponentials(act, t, max_ready, exp_done))

            with phase(f"i{it}_prune") as (block, sem):
                rows_taken, att_ready, chain = sem("rows_taken"), sem("att_ready"), sem("dve_step")
                norm_ready, root, xn_ready, fold_ready = (sem(n) for n in
                                                          ("norm_ready", "root", "xn_ready", "fold_ready"))
                spread_done = sem("spread_done")
                sems = {n: sem(n) for n in SOFT}

                @block.scalar
                def _(act):
                    take_rows(act, 6, rows_taken)
                    global_softmax_scalar(act, sems)
                    act.wait_ge(norm_ready, 1)
                    nc.scalar.activation(st["feat"][:, :], st["feat"][:, :], ACT.Sqrt).then_inc(root, 1)

                @block.gpsimd
                def _(pool):
                    global_softmax_pool(pool, sems)

                @block.tensor
                def _(pe):
                    pe.wait_ge(rows_taken, 4)
                    rows_to_columns(0).then_inc(att_ready, 1)
                    pe.wait_ge(xn_ready, 1)
                    fold(tmp, fold4).then_inc(fold_ready, 1)

                @block.vector
                def _(dve):
                    v = nc.vector
                    do = Chain(dve, chain)
                    do(v.tensor_scalar(st["score"][:, :], st["struct"][:, :], 0.5, None, ALU.mult))
                    dve.wait_ge(att_ready, 1)
                    do(v.tensor_scalar(blocks4(st["mean"]), columns(0), 0.5 / N, None, ALU.mult))
                    do(v.tensor_tensor(st["score"][:, :], st["mean"][:, :], st["score"][:, :], ALU.add))
                    global_softmax_vector(dve, do, sems)
                    do(v.tensor_scalar(st["comp"][:, :], st["score"][:, :], th, None, ALU.is_ge))
                    do(v.tensor_scalar(st["refuse"][:, :], st["comp"][:, :], -REFUSE, REFUSE, ALU.mult, ALU.add))
                    do(v.tensor_tensor(st["feat"][:, :], st["sumsq"][:, :], st["comp"][:, :], ALU.mult))
                    v.tensor_scalar(st["feat"][:, :], st["feat"][:, :], NORM_FLOOR, None, ALU.max)\
                        .then_inc(norm_ready, 1)
                    dve.wait_ge(root, 1)
                    do(v.tensor_scalar(st["var"][:, :], st["feat"][:, :], 1e-8, None, ALU.max))
                    do(v.reciprocal(st["var"][:, :], st["var"][:, :]))
                    do(v.tensor_tensor(st["var"][:, :], st["var"][:, :], st["comp"][:, :], ALU.mult))
                    v.tensor_tensor(tmp[:, :, :], cur[:, :, :], per_node(st["var"]), ALU.mult).then_inc(xn_ready, 1)
                    dve.wait_ge(fold_ready, 1)
                    split(do, fold4)
                    do(spread(v.tensor_copy, sta_a, hi, mid))
                    do(spread(v.tensor_copy, mov_a, hi, hi))
                    do(spread(v.tensor_copy, mov_b, mid, mid))
                    do(spread(v.tensor_copy, sta_b, hi, lo))
                    spread(v.tensor_copy, mov_c, lo, hi).then_inc(spread_done, 1)
                    dve.wait_ge(spread_done, 1)

                loaded = [sem(f"block_loaded{s}") for s in range(SL3)]
                stored = [sem(f"block_stored{s}") for s in range(SL3)]
                scores_ready, chunk_used, max_ready = sem("scores_ready"), sem("chunk_used"), sem("max_ready")
                seen = sem("scores_seen")
                exp_done, cut_ready, pruned = sem("exp_done"), sem("cut_ready"), sem("pruned")

                @block.sync
                def _(sp):
                    def store(t):
                        s = t.slot(SL3)
                        sp.wait_ge(pruned, t.n + 1)
                        sp.dma_start(Hp_rows[t.n], quarters(prod[s])).then_inc(stored[s], 16)

                    def body(t):
                        if t.k >= SL3:
                            store(back(t, SL3))
                        sp.dma_start(held[t.slot(SL3)], adj_b[t.n]).then_inc(loaded[t.slot(SL3)], 16)
                    row_blocks(sp, 3, 5, 0, body)
                    for n in range(NB - SL3, NB):
                        store(Step(n, n, None, 3))
                    for s in range(SL3):
                        sp.wait_ge(stored[s], 16 * len(range(s, NB, SL3)))

                @block.tensor
                def _(pe):
                    pe.wait_ge(spread_done, 1)
                    row_blocks(pe, 3, 5, 0, lambda t: score_products(pe, t, scores_ready, chunk_used))

                @block.vector
                def _(dve):
                    def prune(t):
                        s = t.slot(SL3)
                        dve.wait_ge(exp_done, t.n + 1)
                        nc.vector.scalar_tensor_tensor(
                            out=cut[:, s:s + 1], in0=zsum[:, s:s + 1], scalar=th,
                            in1=st["refuse"][:, bass.ds(t.n, 1)], op0=ALU.mult, op1=ALU.add).then_inc(cut_ready, 1)
                        dve.wait_ge(cut_ready, t.n + 1)
                        nc.vector.scalar_tensor_tensor(
                            out=prod[s], in0=prod[s], scalar=cut[:, s:s + 1], in1=held[s],
                            op0=ALU.is_ge, op1=ALU.mult,
                            accum_out=st["conn"][:, bass.ds(t.n, 1)]).then_inc(pruned, 1)

                    def body(t):
                        s = t.slot(SL3)
                        dve.wait_ge(loaded[s], 16 * (t.turn(SL3) + 1))
                        wait(dve, stored[s], t.turn(SL3) * 16)
                        weighted_scores(dve, t, seen, scores_ready, chunk_used, max_ready)
                        if t.k >= 1:
                            prune(back(t, 1))
                    row_blocks(dve, 3, 5, 0, body)
                    prune(Step(NB - 1, NB - 1, None, 3))

                @block.scalar
                def _(act):
                    row_blocks(act, 3, 5, 0, lambda t: exponentials(act, t, max_ready, exp_done))

            with phase(f"i{it}_gather") as (block, sem):
                moved_ready, chain, deg_floor, deg_root = sem("moved_ready"), sem("dve_step"), sem("deg_floor"), sem("deg_root")
                sems = {n: sem(n) for n in SOFT}

                @block.scalar
                def _(act):
                    global_softmax_scalar(act, sems)
                    act.wait_ge(deg_floor, 1)
                    nc.scalar.activation(st["dv"][:, :], st["dv"][:, :], ACT.Sqrt).then_inc(deg_root, 1)

                @block.gpsimd
                def _(pool):
                    global_softmax_pool(pool, sems)

                @block.vector
                def _(dve):
                    v = nc.vector
                    do = Chain(dve, chain)
                    v.tensor_scalar(st["dv"][:, :], st["conn"][:, :], DEG_EPS, None, ALU.max).then_inc(deg_floor, 1)
                    do(v.tensor_tensor(st["score"][:, :], st["conn"][:, :], st["feat"][:, :], ALU.mult))
                    global_softmax_vector(dve, do, sems)
                    do(v.scalar_tensor_tensor(out=st["node"][:, :], in0=st["score"][:, :], scalar=th,
                                              in1=st["comp"][:, :], op0=ALU.is_ge, op1=ALU.mult))
                    do(v.scalar_tensor_tensor(out=st["node"][:, :], in0=st["conn"][:, :], scalar=0.0,
                                              in1=st["node"][:, :], op0=ALU.is_gt, op1=ALU.mult))
                    dve.wait_ge(deg_root, 1)
                    do(v.reciprocal(st["dv"][:, :], st["dv"][:, :]))
                    do(v.tensor_tensor(st["node"][:, :], st["node"][:, :], st["dv"][:, :], ALU.mult))
                    v.tensor_tensor(moved[:, :, :], xw[:, :, :], per_node(st["node"]), ALU.mult)\
                        .then_inc(moved_ready, 1)

                accumulate(block, sem, Hp_rows, True, (moved_ready, 1), (moved_ready, 1))

            with phase(f"i{it}_scatter") as (block, sem):
                acc_taken, rows_taken, chain = sem("acc_taken"), sem("rows_taken"), sem("dve_step")
                nat_ready, deg_ready, agg_ready = sem("nat_ready"), sem("deg_ready"), sem("agg_ready")

                @block.scalar
                def _(act):
                    take_rows(act, 4, rows_taken)

                @block.tensor
                def _(pe):
                    pe.wait_ge(rows_taken, 4)
                    rows_to_columns(4).then_inc(deg_ready, 1)
                    pe.wait_ge(acc_taken, 1)
                    for b in range(NB):
                        h = b // HB
                        last = nc.tensor.matmul(nat4[:, b, :],
                                                accT[F * h:F * h + F, P * (b % HB):P * (b % HB) + P],
                                                ident[F * h:F * h + F, F * h:F * h + F], start=True, stop=True)
                    last.then_inc(nat_ready, 1)

                @block.vector
                def _(dve):
                    v = nc.vector
                    do = Chain(dve, chain)
                    v.tensor_copy(accT[:, :], fold4).then_inc(acc_taken, 1)
                    dve.wait_ge(deg_ready, 1)
                    do(v.tensor_scalar(blocks4(st["var"]), columns(4), DEG_EPS, None, ALU.max))
                    do(v.reciprocal(st["var"][:, :], st["var"][:, :]))
                    dve.wait_ge(nat_ready, 1)
                    de = per_node(st["var"])
                    for q in range(4):
                        for a in range(4):
                            src, dst = slice(32 * a, 32 * a + 32), slice(32 * q, 32 * q + 32)
                            last = v.tensor_tensor(moved[dst, a::4, :], nat4[src, 8 * q:8 * q + 8, :],
                                                   de[src, 8 * q:8 * q + 8, :], ALU.mult)
                    last.then_inc(agg_ready, 1)

                SL = 4
                loaded = [sem(f"block_loaded{s}") for s in range(SL)]
                turned_done, msg_ready, msg_taken, out_ready, out_taken = (
                    sem(n) for n in ("turned", "msg_ready", "msg_taken", "out_ready", "out_taken"))
                turned = [stream[:, 4 + s, :] for s in range(2)]

                @block.sync
                def _(sp):
                    def body(t):
                        wait(sp, turned_done, t.n - (SL - 1))
                        sp.dma_start(stream[:, t.slot(SL), :], Hp_quarters[t.n]).then_inc(loaded[t.slot(SL)], 16)
                    row_blocks(sp, 4, 4, 0, body)

                @block.tensor
                def _(pe):
                    pe.wait_ge(agg_ready, 1)

                    def gather(t):
                        s = t.slot(2)
                        pe.wait_ge(turned_done, t.n + 1)
                        wait(pe, msg_taken, t.n - 1)
                        view = turned[s].rearrange("p (g b r) -> p b g r", g=4, r=32)
                        for b in range(NB):
                            h = b % 2
                            last = nc.tensor.matmul(ps[F * h:F * h + F, 4 + s, 0:P], moved[:, b, :], view[:, b, :, :],
                                                    start=b < 2, stop=b >= NB - 2, skip_group_check=True)
                        last.then_inc(msg_ready, 1)

                    def finish(t):
                        s = t.slot(2)
                        pe.wait_ge(msg_taken, t.n + 1)
                        wait(pe, out_taken, t.n - 1)
                        nc.tensor.matmul(ps[:, 6 + s, 0:F], msgT[:, s, :], theta[:, :],
                                         start=True, stop=True).then_inc(out_ready, 1)

                    def body(t):
                        gather(t)
                        if t.k >= 1:
                            finish(back(t, 1))
                    row_blocks(pe, 4, 4, 0, body)
                    finish(Step(NB - 1, NB - 1, None, 4))

                @block.scalar
                def _(act):
                    def message(t):
                        s = t.slot(2)
                        act.wait_ge(msg_ready, t.n + 1)
                        wait(act, out_ready, t.n - 1)
                        by_node = ps[:, 4 + s, 0:P].rearrange("p (g r) -> p r g", g=4)
                        nc.scalar.copy(msgT[:, s, :].rearrange("p (r g) -> p r g", g=4), by_node)\
                            .then_inc(msg_taken, 1)

                    def output(t):
                        s = t.slot(2)
                        act.wait_ge(out_ready, t.n + 1)
                        dst = cur[:, bass.ds(t.n, 1), :].rearrange("p a f -> p (a f)")
                        nc.scalar.activation(dst, ps[:, 6 + s, 0:F], ACT.Relu,
                                             scale=st["dv"][:, bass.ds(t.n, 1)]).then_inc(out_taken, 1)

                    def body(t):
                        message(t)
                        if t.k >= 1:
                            output(back(t, 1))
                    row_blocks(act, 4, 4, 0, body)
                    output(Step(NB - 1, NB - 1, None, 4))

                @block.vector
                def _(dve):
                    def body(t):
                        dve.wait_ge(loaded[t.slot(SL)], 16 * (t.turn(SL) + 1))
                        wait(dve, msg_ready, t.n - 1)
                        nc.vector.transpose(turned[t.slot(2)], stream[:, t.slot(SL), :]).then_inc(turned_done, 1)
                    row_blocks(dve, 4, 4, 0, body)

            if not last_it:
                with phase(f"i{it + 1}_edge") as (block, sem):
                    cur_ready = sem("cur_ready")

                    @block.vector
                    def _(dve):
                        dve.sem_inc(cur_ready, 1)

                    edge_pass(block, sem, (cur_ready, 1))

        sup_all = streamb[:, 0:3 * HALF].rearrange("p (n t f) -> p n t f", t=3, f=F)
        with phase("l3") as (block, sem):
            x_ready, fold_ready, fold_taken, sup_ready, chain, sup_split = (
                sem(n) for n in ("x_ready", "fold_ready", "fold_taken", "sup_ready", "dve_step", "support_split"))
            var_ready, std_ready = sem("var_ready"), sem("std_ready")

            @block.scalar
            def _(act):
                root_of_variance(act, var_ready, std_ready)

            @block.tensor
            def _(pe):
                pe.wait_ge(x_ready, 1)
                fold(res, fold4).then_inc(fold_ready, 1)
                pe.wait_ge(fold_taken, 1)
                project(nat4, curT, w3).then_inc(sup_ready, 1)

            @block.vector
            def _(dve):
                v = nc.vector
                do = Chain(dve, chain)
                do(v.tensor_tensor(res[:, :, :], res[:, :, :], cur[:, :, :], ALU.add))
                layer_norm(dve, do, res, res, var_ready, std_ready)
                v.tensor_copy(tmp[:, :, :], res[:, :, :]).then_inc(x_ready, 1)
                dve.wait_ge(fold_ready, 1)
                v.tensor_copy(curT[:, :], fold4).then_inc(fold_taken, 1)
                dve.wait_ge(sup_ready, 1)
                do(v.tensor_scalar(tmp[:, :, :], nat4, 2.0, None, ALU.mult))
                do(v.tensor_copy(sup_all[:, :, 0, :], tmp[:, :, :]))
                do(v.tensor_tensor(tmp[:, :, :], tmp[:, :, :], sup_all[:, :, 0, :], ALU.subtract))
                do(v.tensor_copy(sup_all[:, :, 1, :], tmp[:, :, :]))
                v.tensor_tensor(sup_all[:, :, 2, :], tmp[:, :, :], sup_all[:, :, 1, :], ALU.subtract)\
                    .then_inc(sup_split, 1)

            SL = 4
            loaded = [sem(f"block_loaded{s}") for s in range(SL)]
            masked, scanned, edges = sem("masked"), sem("scanned"), sem("edges_set")
            diff_ready, diff_taken, sum_ready, sum_taken = (sem(n) for n in
                                                            ("diff_ready", "diff_taken", "sum_ready", "sum_taken"))
            factor = [mov_a[:, :], mov_b[:, :]]
            decay = [streamb[:, 3 * HALF + (N + 2) * s:3 * HALF + (N + 2) * s + N + 1] for s in range(2)]
            weight = [mov_c[:, :], sta_a[:, :]]

            @block.sync
            def _(sp):
                def body(t):
                    wait(sp, masked, t.n - (SL - 1))
                    sp.dma_start(stream[:, t.slot(SL), :], adj_b[t.n]).then_inc(loaded[t.slot(SL)], 16)
                row_blocks(sp, 4, 4, 0, body)

            @block.vector
            def _(dve):
                v = nc.vector
                for s in range(2):
                    v.memset(decay[s][:, N:N + 1], 1.0).then_inc(edges, 1)

                def output(t):
                    dve.wait_ge(sum_ready, t.n + 1)
                    dst = cur[:, bass.ds(t.n, 1), :].rearrange("p a f -> p (a f)")
                    parts = ps[:, 6 + t.slot(2), 0:3 * F].rearrange("p (t f) -> p f t", t=3)
                    v.reduce_sum(dst, parts, AX.X).then_inc(sum_taken, 1)

                def body(t):
                    s = t.slot(2)
                    dve.wait_ge(loaded[t.slot(SL)], 16 * (t.turn(SL) + 1))
                    wait(dve, scanned, t.n - 1)
                    v.tensor_scalar(factor[s], stream[:, t.slot(SL), :], 0.0, 0.5, ALU.is_equal, ALU.max)\
                        .then_inc(masked, 1)
                    dve.wait_ge(masked, t.n + 1)
                    wait(dve, diff_ready, t.n * NC - NC)
                    v.tensor_tensor_scan(decay[s][:, N - 1::-1], factor[s][:, ::-1],
                                         floor_w[:, :].to_broadcast([P, N]), 1.0,
                                         ALU.mult, ALU.max).then_inc(scanned, 1)
                    if t.k >= 2:
                        output(back(t, 2))
                row_blocks(dve, 4, 4, 0, body)
                for n in (NB - 2, NB - 1):
                    output(Step(n, n, None, 4))

            @block.tensor
            def _(pe):
                pe.wait_ge(edges, 2)
                pe.wait_ge(sup_split, 1)

                def combine(t):
                    s = t.slot(2)
                    pe.wait_ge(diff_taken, t.n * NC + NC)
                    wait(pe, sum_taken, t.n - 1)
                    for jb in range(NB):
                        last = nc.tensor.matmul(ps[:, 6 + s, 0:3 * F], weight[s][:, P * jb:P * jb + P],
                                                sup_all[:, jb, :, :].rearrange("p t f -> p (t f)"),
                                                start=jb == 0, stop=jb == NB - 1)
                    last.then_inc(sum_ready, 1)

                def body(t):
                    s = t.slot(2)
                    pe.wait_ge(scanned, t.n + 1)
                    for q in range(NC):
                        wait(pe, diff_taken, t.n * NC + (q - 1))
                        for i in range(8):
                            jb = 8 * q + i
                            out = ps[:, 2 * (q % 2) + i // 4, P * (i % 4):P * (i % 4) + P]
                            nc.tensor.matmul(out, decay[s][:, P * jb + 1:P * jb + 1 + P], ident_b[:, :],
                                             start=True, stop=False)
                            last = nc.tensor.matmul(out, decay[s][:, P * jb:P * jb + P], neg_ident_b[:, :],
                                                    start=False, stop=True)
                        last.then_inc(diff_ready, 1)
                    if t.k >= 1:
                        combine(back(t, 1))
                row_blocks(pe, 4, 4, 0, body)
                combine(Step(NB - 1, NB - 1, None, 4))

            @block.scalar
            def _(act):
                def body(t):
                    for q in range(NC):
                        act.wait_ge(diff_ready, t.n * NC + (q + 1))
                        wait(act, sum_ready, t.n - 1)
                        nc.scalar.copy(weight[t.slot(2)][:, CHUNK * q:CHUNK * q + CHUNK],
                                       ps[:, 2 * (q % 2):2 * (q % 2) + 2, :].rearrange("p a b -> p (a b)"))\
                            .then_inc(diff_taken, 1)
                row_blocks(act, 4, 4, 0, body)

        with phase("out") as (block, sem):
            chain, out_stored, out_made = sem("dve_step"), sem("out_stored"), sem("out_made")
            var_ready, std_ready = sem("var_ready"), sem("std_ready")

            @block.scalar
            def _(act):
                root_of_variance(act, var_ready, std_ready)

            @block.vector
            def _(dve):
                v = nc.vector
                do = Chain(dve, chain)
                do(v.tensor_tensor(cur[:, :, :], cur[:, :, :], per_feature(b3), ALU.add))
                do(v.tensor_tensor(cur[:, :, :], cur[:, :, :], res[:, :, :], ALU.add))
                layer_norm(dve, do, cur, cur, var_ready, std_ready)
                v.tensor_copy(res[:, :, :], cur[:, :, :]).then_inc(out_made, 1)

            @block.sync
            def _(sp):
                sp.wait_ge(out_made, 1)
                sp.dma_start(d["out"].rearrange("(n p) f -> p n f", p=P), res[:, :, :]).then_inc(out_stored, 16)
                sp.wait_ge(out_stored, 16)


def kernel(**inputs):
    import numpy as np
    import concourse.bacc as bacc
    from concourse.bass_utils import run_bass_kernel_spmd as run

    nc = bacc.Bacc("TRN2", target_bir_lowering=False, num_devices=1)
    adj = np.asarray(inputs["adj"])
    x = np.asarray(inputs["x"])
    arrays = {
        "x": x, "xT": x.T, "adj": adj, "adjT": adj.T,
        "W0": inputs["L0_gnn_W"], "b0": inputs["L0_gnn_b"], "W1T": np.asarray(inputs["L1_gnn_W"]).T,
        "W": inputs["L2_gnn_W"], "Theta": inputs["L2_gnn_Theta"], "Wq": inputs["L2_gnn_Wq"],
        "bq": inputs["L2_gnn_bq"], "Wv": inputs["L2_gnn_Wv"], "bv": inputs["L2_gnn_bv"],
        "W3": inputs["L3_gnn_weight"], "b3": inputs["L3_gnn_bias"],
    }
    arrays = {n: np.ascontiguousarray(a) for n, a in arrays.items()}
    d = {n: nc.dram_tensor(f"in_{n}", a.shape, F32, kind="ExternalInput").ap() for n, a in arrays.items()}
    d["out"] = nc.dram_tensor("out", (N, F), F32, kind="ExternalOutput").ap()
    build(nc, d)
    r = run(nc, [{f"in_{n}": a for n, a in arrays.items()}], core_ids=[0])
    return r.results[0]["out"]
```

```python
import concourse.bass as bass
from concourse import mybir
from contextlib import ExitStack, contextmanager
import numpy as np

F32 = mybir.dt.float32
BF16 = mybir.dt.bfloat16
ALU = mybir.AluOpType
ACT = mybir.ActivationFunctionType
AX = mybir.AxisListType

P = 128
N = 4096
F = 64
NB = N // P
HALF = N // 2
HB = NB // 2
BANK = 512
LN_EPS = 1e-5
DEG_EPS = 1e-6
NORM_FLOOR = 1e-16
FEAT_FLOOR = 1e-8
NEG_HUGE = -3.0e38
REFUSE = 1.0e30
W_FLOOR = 2.0 ** -100
THETAS = [0.000244 + (1.0 - float(np.exp(-0.1 * it))) * (0.0003 - 0.000244) for it in range(2)]


class Step:

    def __init__(self, n, k, it, unroll, seq):
        self.n, self.k, self.it, self.unroll, self.seq = n, k, it, unroll, seq
        self.block = seq[n] if it is None else n + (seq[k] - k)

    def back(self, by):
        return Step(self.n - by, self.k - by, self.it, self.unroll, self.seq)

    def turn(self, slots, resident=0):
        before = len([m for m in range(resident, self.k) if (self.k - m) % slots == 0])
        return before if self.it is None else self.it * (self.unroll // slots) + before


def row_blocks(e, unroll, lead, body, seq=range(32)):
    groups = (NB - lead) // unroll
    assert lead + groups * unroll == NB
    assert len({seq[n] - n for n in range(lead, NB)}) == 1
    for n in range(lead):
        body(Step(n, n, None, unroll, seq))
    with e.Fori(0, groups) as it:
        for u in range(unroll):
            body(Step(it * unroll + (lead + u), lead + u, it, unroll, seq))


def last_step(n, seq=range(32)):
    return Step(n, n, None, 1, seq)


def wait(e, sem, value):
    if isinstance(value, int) and value <= 0:
        return
    e.wait_ge(sem, value)


def build(nc, d):
    ctx = ExitStack()
    with ctx:
        def sb(name, shape, dt=F32):
            return ctx.enter_context(nc.sbuf_tensor(name, shape, dt))

        ps = ctx.enter_context(nc.psum_tensor("ps", [P, 8, BANK], F32))
        res = sb("res", [P, NB, F])
        moved = sb("moved", [P, NB, F])
        xw = sb("xw", [P, NB, F])
        spare = sb("spare", [P, 2, NB, F])
        cur = spare[:, 0, :, :]
        tmp = spare[:, 1, :, :]
        spare_block = spare[:, :, :, :].rearrange("p s n f -> p (s n f)")
        accT = sb("accT", [P, HALF])
        curT = sb("curT", [P, HALF])
        rows = sb("rows", [P, 2 * BANK])
        mov_ab = sb("mov_ab", [P, 2, N], BF16)
        mov_a = mov_ab[:, 0, :]
        mov_b = mov_ab[:, 1, :]
        mov_c = sb("mov_c", [P, N], BF16)
        sta_ab = sb("sta_ab", [P, 2, N], BF16)
        sta_a = sta_ab[:, 0, :]
        sta_b = sta_ab[:, 1, :]
        stage = sb("stage", [P, 8, F])
        ident = sb("ident", [P, P])
        centre_w = sb("centre_w", [P, P])
        ident_b = sb("ident_b", [P, P], BF16)
        comp_b = sb("comp_b", [P, NB], BF16)
        neg_ident_b = sb("neg_ident_b", [P, P], BF16)
        ones = sb("ones", [P, 1])
        zeros_b = sb("zeros_b", [P, BANK], BF16)
        floor_w = sb("floor_w", [P, 1])
        twice = sb("twice", [P, 7, P])
        w0, w1s, w1n, wq, wv, w2, w3 = (twice[:, i, :] for i in range(7))
        theta = sb("theta", [P, F])
        bv, b3 = (sb(n, [P, F]) for n in ("bv", "b3"))
        bq8 = sb("bq8", [P, 1])
        b0 = sb("b0", [P, 1])
        st = {n: sb(n, [P, NB]) for n in ("mean", "var", "std", "rdeg", "struct", "norm", "rnorm", "comp", "feat",
                                          "refuse", "conn", "dv", "score", "node")}
        gl = {n: sb(n, [P, 1]) for n in ("gmax", "gmaxall", "gneg", "gsum", "gsumall", "grec")}
        mx4 = sb("mx4", [P, 3, 4])
        negmax = sb("negmax", [P, 3])
        zsum = sb("zsum", [P, 3])
        rz = sb("rz", [P, 3])
        cut = sb("cut", [P, 3])
        msgT = stage[:, 0:4, :].rearrange("p (s a) f -> p s (a f)", s=2)
        stream = sb("stream", [P, 6, N])
        slot = [*(stream[:, s, :] for s in range(6)),
                *(t[:, :, :].rearrange("p a n -> p (a n)").bitcast(F32) for t in (mov_ab, sta_ab))]
        streamb = stream[:, 4:6, :].rearrange("p s n -> p (s n)").bitcast(BF16)

        Hp = nc.dram_tensor("pruned", (NB, 4, P, N // 4), F32, kind="Internal").ap()
        Hp_rows = Hp.rearrange("n q p j -> n p q j")
        Hp_quarters = Hp.rearrange("n q (r g) j -> n (q r) (g j)", g=4)

        def by_rows(m):
            return m.rearrange("(n p) c -> n p c", p=P)

        adj_b, adjT_b = by_rows(d["adj"]), by_rows(d["adjT"])

        def quarters(a):
            return a.rearrange("p (q j) -> p q j", q=4)

        @contextmanager
        def phase(name, ahead=()):
            made = list(ahead)

            def sem(n):
                s = nc.alloc_semaphore(f"{name}_{n}")
                made.append(s)
                return s

            with nc.Block() as block:
                yield block, sem
            nc.clear_and_free_semaphores(made)
            nc.all_engine_barrier()

        def loads_ahead(name):
            return [nc.alloc_semaphore(f"{name}_row_block_loaded{s}") for s in range(4)]

        nat4 = ps[:, 0:4, :].rearrange("p b (k f) -> p (b k) f", f=F)
        nat4b = ps[:, 4:8, :].rearrange("p b (k f) -> p (b k) f", f=F)
        fold4 = ps[:, 0:4, :].rearrange("p b c -> p (b c)")
        fold4b = ps[:, 4:8, :].rearrange("p b c -> p (b c)")

        def per_node(a):
            return a[:, :].unsqueeze(2).to_broadcast([P, NB, F])

        def per_node_part(a, k):
            return part(a, k).unsqueeze(2).to_broadcast([P, QB, F])

        def per_feature(a, blocks=NB):
            return a[:, :].unsqueeze(1).to_broadcast([P, blocks, F])

        def even_odd(a):
            return a.rearrange("p (c h q) -> p h c q", h=2, q=P)

        def pairs(a):
            return a.rearrange("p (c h) f -> p c (h f)", h=2)

        def project(dst, srcT, w, parts=None, before=lambda k: None):
            for c in range(HB):
                if c % 4 == 0:
                    before(c // 4)
                last = nc.tensor.matmul(pairs(dst)[:, c, :], srcT[:, P * c:P * c + P], w[:, :], start=True, stop=True)
                if parts is not None and c % 4 == 3:
                    last.then_inc(parts, 1)
            return last

        def fold(src, dst, parts=None, before=lambda k: None):
            for c in range(HB):
                if c % 4 == 0:
                    before(c // 4)
                last = nc.tensor.transpose(dst[:, P * c:P * c + P], pairs(src)[:, c, :], ident[:, :])
                if parts is not None and c % 4 == 3:
                    last.then_inc(parts, 1)
            return last

        def unfold(srcT, dst, parts):
            for c in range(HB):
                last = nc.tensor.transpose(pairs(dst)[:, c, :], srcT[:, P * c:P * c + P], ident[:, :])
                if c % 4 == 3:
                    last.then_inc(parts, 1)

        def rows_to_columns(bank):
            for m in range(8):
                last = nc.tensor.matmul(ps[:, bank, 4 * m:4 * m + 4], rows[:, P * m:P * m + P], ident[:, 0::32],
                                        start=True, stop=True)
            return last

        def columns(bank):
            return ps[:, bank, 0:NB].rearrange("p (j i g) -> p j g i", j=2, i=4)

        def blocks4(a):
            return a[:, :].rearrange("p (j g i) -> p j g i", j=2, g=4)

        class Chain:

            def __init__(self, e, sem):
                self.e, self.sem, self.count = e, sem, 0

            def __call__(self, ins):
                self.count += 1
                ins.then_inc(self.sem, 1)
                self.e.wait_ge(self.sem, self.count)

        QB = NB // 4

        def part(a, k):
            return a[:, QB * k:QB * k + QB]

        class LayerNorm:

            def __init__(self, sem):
                self.centred, self.squared = sem("centred"), sem("squared")
                self.var_ready, self.std_ready = sem("var_ready"), sem("std_ready")

            def scalar(self, act, centred):
                for k in range(4):
                    act.wait_ge(self.centred, k + 1)
                    nc.scalar.activation(part(tmp, k), part(centred, k), ACT.Square).then_inc(self.squared, 1)
                self.root(act)

            def root(self, act):
                act.wait_ge(self.var_ready, 1)
                nc.scalar.activation(st["std"][:, :], st["var"][:, :], ACT.Sqrt).then_inc(self.std_ready, 1)

            def centre(self, do, y):
                v = nc.vector
                for k in range(4):
                    do(v.reduce_sum(part(st["mean"], k), part(y, k), AX.X))
                    do(v.tensor_scalar(part(st["mean"], k), part(st["mean"], k), 1.0 / F, None, ALU.mult))
                    v.tensor_tensor(part(y, k), part(y, k),
                                    per_node_part(st["mean"], k), ALU.subtract)\
                        .then_inc(self.centred, 1)

            def variances(self, dve, do):
                for k in range(4):
                    dve.wait_ge(self.squared, k + 1)
                    last = nc.vector.reduce_sum(part(st["var"], k), part(tmp, k), AX.X)
                do(last)

            def scale(self, dve, do, dst, centred, made):
                v = nc.vector
                v.tensor_scalar(st["var"][:, :], st["var"][:, :], 1.0 / F, LN_EPS, ALU.mult, ALU.add)\
                    .then_inc(self.var_ready, 1)
                dve.wait_ge(self.std_ready, 1)
                do(v.reciprocal(st["std"][:, :], st["std"][:, :]))
                for k in range(4):
                    v.tensor_tensor(part(dst, k), part(centred, k), per_node_part(st["std"], k), ALU.mult)\
                        .then_inc(made, 1)

        TOP, LOW = slice(0, F), slice(F, P)
        edge_rest = mov_a[:, :].bitcast(F32)
        edge_parts = mov_b[:, 0:HALF], mov_b[:, HALF:N], mov_c[:, 0:HALF]
        rest = stream[:, 5, HALF:N]
        hi, mid, lo = (streamb[:, N + HALF * i:N + HALF * i + HALF] for i in range(3))

        xn_hi, xn_mid = (accT[:, :].bitcast(BF16)[:, HALF * i:HALF * i + HALF] for i in range(2))
        xn_lo = curT[:, :].bitcast(BF16)[:, 0:HALF]

        def split(do, src, rest, hi, mid, lo):
            v = nc.vector
            do(v.tensor_copy(hi, src))
            do(v.tensor_tensor(rest, src, hi, ALU.subtract))
            do(v.tensor_copy(mid, rest))
            do(v.tensor_tensor(lo, rest, mid, ALU.subtract))

        def bank_of(a, k):
            return a[:, BANK * k:BANK * k + BANK]

        def spread_bank(copy, dst, top, low, k):
            for part, rows_out in ((top, TOP), (low, LOW)):
                for h in range(2):
                    last = copy(even_odd(dst[rows_out, :])[:, h, 4 * k:4 * k + 4],
                                bank_of(part[F * h:F * h + F, :], k).rearrange("p (c q) -> p c q", q=P))
            return last

        def spread_rows(copy, dst, rows_out, folded):
            for h in range(2):
                last = copy(even_odd(dst[rows_out, :])[:, h],
                            folded[F * h:F * h + F, :].rearrange("p (c q) -> p c q", q=P))
            return last

        def spread(copy, dst, top, low):
            spread_rows(copy, dst, TOP, top)
            return spread_rows(copy, dst, LOW, low)

        def in_order(a, c):
            return a[:, BANK * c:BANK * c + BANK]

        def in_turned_order(a, c):
            return a.rearrange("p (q s i) -> p s q i", q=4, i=32)[:, 4 * c:4 * c + 4]

        def accumulate(block, sem, matrix_b, column_sums, moved_ready, banks_free, side={}, scalar_side={},
                       seq=range(NB), slots=(0, 1, 2, 3, 4, 5), resident=0, issued=0, loaded=(), lead=8, ahead=(),
                       bank=0):
            SL = len(slots)
            loaded = [*loaded, *(sem(f"row_block_loaded{s}") for s in range(len(loaded), SL))]
            staged = sem("stationary_staged")
            used = sem("row_block_used")
            added = sem("row_block_added")

            @block.sync
            def _(sp):
                def body(t):
                    if t.k < max(resident, issued):
                        return
                    wait(sp, used, t.n - (SL - 1))
                    if column_sums:
                        wait(sp, added, t.n - (SL - 1))
                    dst = slot[slots[t.k % SL]]
                    if matrix_b is Hp_rows:
                        dst = quarters(dst)
                    sp.dma_start(dst, matrix_b[t.block]).then_inc(loaded[t.k % SL], 16)
                row_blocks(sp, SL, lead, body, seq)
                for steps, dst, source, begun in ahead:
                    sp.wait_ge(used, steps)
                    if column_sums:
                        sp.wait_ge(added, steps)
                    sp.dma_start(dst, source).then_inc(begun, 16)

            @block.scalar
            def _(act):
                act.wait_ge(*moved_ready)

                def body(t):
                    wait(act, used, t.n - (SL - 1))
                    nc.scalar.activation(stage[:, t.k % SL, :], natural_block(moved, t.block), ACT.Copy)\
                        .then_inc(staged, 1)
                    if t.it is None and t.k in scalar_side:
                        scalar_side[t.k](act)
                row_blocks(act, SL, lead, body, seq)

            @block.tensor
            def _(pe):
                pe.wait_ge(*banks_free)
                for b in range(4):
                    for h in range(2):
                        nc.tensor.matmul(ps[F * h:F * h + F, bank + b, :], zeros_b[:, 0:F], zeros_b[:, :],
                                         start=True, stop=False, skip_group_check=True)

                def body(t):
                    src = slot[slots[t.k % SL]]
                    if t.k >= resident:
                        pe.wait_ge(loaded[t.k % SL], 16 * (t.turn(SL, resident) + 1))
                    pe.wait_ge(staged, t.n + 1)
                    for b in range(4):
                        for h in range(2):
                            last = nc.tensor.matmul(ps[F * h:F * h + F, bank + b, :], stage[:, t.k % SL, :],
                                                    even_odd(src)[:, h, 4 * b:4 * b + 4, :], start=False,
                                                    stop=False, skip_group_check=True)
                    last.then_inc(used, 1)
                    if t.it is None and t.k in side:
                        side[t.k](pe)
                row_blocks(pe, SL, lead, body, seq)
                if column_sums:
                    pe.wait_ge(added, NB)
                    for c in range(8):
                        g, j = c % 4, c // 4
                        nc.tensor.matmul(ps[32 * g:32 * g + 1, 4 + j, :], ones[:, :],
                                         column_sums(spare_block, c), start=True, stop=True)

            if not column_sums:
                return

            @block.vector
            def _(dve):
                def body(t):
                    src = slot[slots[t.k % SL]]
                    if t.k >= resident:
                        dve.wait_ge(loaded[t.k % SL], 16 * (t.turn(SL, resident) + 1))
                    wait(dve, added, t.n)
                    if t.it is None and t.k == 0:
                        nc.vector.tensor_copy(spare_block, src).then_inc(added, 1)
                    else:
                        nc.vector.tensor_tensor(spare_block, src, spare_block, ALU.add).then_inc(added, 1)
                row_blocks(dve, SL, lead, body, seq)

        def edge_pass(block, sem, src, src_ready, begun=()):
            fold_ready, fold_taken, v_ready, v_taken = (sem(n) for n in
                                                        ("cur_folded", "cur_taken", "v_ready", "v_taken"))
            xw_ready, xw_taken, q_ready, q_taken = (sem(n) for n in ("xw_ready", "xw_taken", "q_ready", "q_taken"))
            norm_ready, root, chain = sem("norm_ready"), sem("root"), sem("edge_step")
            xn_ready, xn_folded = sem("xn_ready"), sem("xn_folded")

            @block.tensor
            def _(pe):
                fold(src, fold4b, fold_ready, before=lambda k: pe.wait_ge(*src_ready[k]))
                project(nat4, curT, wv, v_ready, before=lambda k: pe.wait_ge(fold_taken, k + 1))

            @block.scalar
            def _(act):
                for k in range(4):
                    act.wait_ge(fold_ready, k + 1)
                    nc.scalar.copy(bank_of(curT, k), bank_of(fold4b, k)).then_inc(fold_taken, 1)

            @block.vector
            def _(dve):
                v = nc.vector
                do = Chain(dve, chain)
                for k in range(4):
                    dve.wait_ge(v_ready, k + 1)
                    v.tensor_tensor(part(moved, k), part(nat4, k), per_feature(bv, QB), ALU.add).then_inc(v_taken, 1)
                dve.wait_ge(xw_ready, 1)
                v.tensor_copy(xw[:, :, :], nat4).then_inc(xw_taken, 1)
                dve.wait_ge(q_ready, 1)
                v.tensor_scalar(accT[:, :], fold4, 0.125, bq8[:, :], ALU.mult, ALU.add).then_inc(q_taken, 1)
                dve.wait_ge(q_taken, 1)
                split(do, accT[:, :], edge_rest, *edge_parts)
                q_hi, q_mid, q_lo = edge_parts
                do(spread(v.tensor_copy, sta_a, q_hi, q_mid))
                do(spread(v.tensor_copy, sta_b, q_hi, q_lo))
                do(v.tensor_tensor(tmp[:, :, :], xw[:, :, :], xw[:, :, :], ALU.mult))
                do(v.reduce_sum(st["struct"][:, :], tmp[:, :, :], AX.X))
                v.tensor_scalar(st["struct"][:, :], st["struct"][:, :], NORM_FLOOR, None, ALU.max)\
                    .then_inc(norm_ready, 1)
                do(v.tensor_tensor(tmp[:, :, :], src[:, :, :], src[:, :, :], ALU.mult))
                do(v.reduce_sum(st["norm"][:, :], tmp[:, :, :], AX.X))
                v.tensor_scalar(st["norm"][:, :], st["norm"][:, :], NORM_FLOOR, None, ALU.max)\
                    .then_inc(norm_ready, 1)
                dve.wait_ge(root, 2)
                do(v.reciprocal(st["rnorm"][:, :], st["norm"][:, :]))
                v.tensor_tensor(tmp[:, :, :], src[:, :, :], per_node(st["rnorm"]), ALU.mult).then_inc(xn_ready, 1)
                dve.wait_ge(xn_folded, 1)
                split(do, fold4, edge_rest, xn_hi, xn_mid, xn_lo)

            def side(pe):
                pe.wait_ge(v_taken, 4)
                project(nat4, curT, w2).then_inc(xw_ready, 1)
                pe.wait_ge(xw_taken, 1)
                for b in range(4):
                    last = nc.tensor.matmul(ps[:, b, :], wq[:, :], curT[:, BANK * b:BANK * b + BANK],
                                            start=True, stop=True)
                last.then_inc(q_ready, 1)

            def roots(act):
                for i, n in enumerate(("struct", "norm")):
                    act.wait_ge(norm_ready, i + 1)
                    nc.scalar.activation(st[n][:, :], st[n][:, :], ACT.Sqrt).then_inc(root, 1)

            def fold_xn(pe):
                pe.wait_ge(xn_ready, 1)
                fold(tmp, fold4).then_inc(xn_folded, 1)

            accumulate(block, sem, adj_b, None, (v_taken, 4), (fold_taken, 4), {3: side, 13: fold_xn},
                       {9: roots}, issued=len(begun), loaded=begun, lead=14, bank=4)

        def natural_block(a, b):
            return a[:, bass.ds(b, 1), :].rearrange("p a f -> p (a f)")

        def take_rows(copy, base, groups, taken):
            for g in groups:
                copy(rows[32 * g:32 * g + 1, :], ps[32 * g:32 * g + 1, base:base + 2, :].rearrange("p a b -> p (a b)"))\
                    .then_inc(taken, 1)

        with phase("l0") as (block, sem):
            small_loaded, ident_zero, ident_made = sem("small_loaded"), sem("ident_zero"), sem("ident_made")
            h_ready, h_taken, chain = sem("h_ready"), sem("h_taken"), sem("dve_step")
            loads = []
            first_loads, first_diagonal = [], []
            for h in range(2):
                r = slice(F * h, F * h + F)
                x_half = d["xT"].rearrange("f (c h q) -> h f c q", h=2, q=P)[h]
                first_loads += [(curT[r, :].rearrange("p (c q) -> p c q", q=P), x_half)]
                first_diagonal += [(w0[r, r], d["W0"])]
                loads += [(w[r, r], m) for w, m in ((w1s, d["W1T"][0:F, :]), (w1n, d["W1T"][F:P, :]), (wq, d["Wq"]),
                                                    (wv, d["Wv"]), (w2, d["W"]), (w3, d["W3"]))]
                loads += [(theta[r, :], d["Theta"]), (bq8[r, :], d["bq"].rearrange("(f a) -> f a", a=1)),
                          (b0[r, :], d["b0"].rearrange("(f a) -> f a", a=1))]
            for t, n in ((bv, "bv"), (b3, "b3")):
                loads += [(t[:, :], d[n].rearrange("(a f) -> a f", a=1).broadcast_to([P, F]))]
            loads += [(res[:, :, :], d["x"])]
            first_loaded = sem("first_loaded")
            twice_zero = sem("twice_zero")

            @block.sync
            def _(sp):
                for dst, src in first_loads:
                    sp.dma_start(dst, src).then_inc(first_loaded, 16)
                sp.wait_ge(twice_zero, 1)
                for dst, src in first_diagonal:
                    sp.dma_start(dst, src).then_inc(first_loaded, 16)

            def load_three(k):
                def load(act):
                    for dst, src in loads[3 * k:3 * k + 3]:
                        act.dma_start(dst, src).then_inc(small_loaded, 16)
                return load

            @block.gpsimd
            def _(pool):
                nc.gpsimd.memset(ident[:, :], 0.0).then_inc(ident_zero, 1)
                pool.wait_ge(ident_zero, 1)
                nc.gpsimd.affine_select(out=ident[:, :], in_=ident[:, :], compare_op=ALU.not_equal, fill=1.0,
                                        base=0, pattern=[[-1, P]], channel_multiplier=1).then_inc(ident_made, 1)

            @block.tensor
            def _(pe):
                pe.wait_ge(first_loaded, 16 * len(first_loads + first_diagonal))
                project(nat4, curT, w0).then_inc(h_ready, 1)

            @block.vector
            def _(dve):
                v = nc.vector
                do = Chain(dve, chain)
                v.memset(twice[:, :, :], 0.0).then_inc(twice_zero, 1)
                do(v.memset(centre_w[:, :], 0.0))
                do(v.memset(rows[:, :], 0.0))
                do(v.memset(ones[:, :], 1.0))
                do(v.memset(zeros_b[:, :], 0.0))
                do(v.memset(floor_w[:, :], W_FLOOR))
                dve.wait_ge(ident_made, 1)
                do(v.tensor_copy(ident_b[:, :], ident[:, :]))
                do(v.tensor_scalar(neg_ident_b[:, :], ident[:, :], -1.0, None, ALU.mult))
                for h in range(2):
                    r = slice(F * h, F * h + F)
                    do(v.tensor_scalar(centre_w[r, r], ident[r, r], -1.0 / F, None, ALU.add))
                dve.wait_ge(h_ready, 1)
                v.tensor_copy(moved[:, :, :], nat4).then_inc(h_taken, 1)

            groups = (len(loads) + 2) // 3
            accumulate(block, sem, adjT_b, in_order, (h_taken, 1), (h_taken, 1),
                       scalar_side={k: load_three(k) for k in range(groups)}, slots=range(8))

            @block.vector
            def _(dve):
                v = nc.vector
                dve.wait_ge(small_loaded, 16 * len(loads))
                v.tensor_scalar(bq8[:, :], bq8[:, :], 0.125, None, ALU.mult)
                v.tensor_scalar(w3[:, :], w3[:, :], 2.0, None, ALU.mult)

        with phase("l1") as (block, sem):
            acc_taken, rows_taken, chain = sem("acc_taken"), sem("rows_taken"), sem("dve_step")
            deg_ready, deg_taken, x_made = sem("deg_ready"), sem("deg_taken"), sem("x_made")
            fold_ready, fold_taken, self_ready = sem("fold_ready"), sem("fold_taken"), sem("self_ready")
            res_copied = sem("res_copied")
            norm = LayerNorm(sem)

            @block.scalar
            def _(act):
                norm.scalar(act, nat4)
                take_rows(nc.scalar.copy, 4, range(4), rows_taken)

            @block.tensor
            def _(pe):
                pe.wait_ge(acc_taken, 4)
                project(nat4, accT, centre_w, norm.centred)

            @block.vector
            def _(dve):
                v = nc.vector
                do = Chain(dve, chain)
                for b in range(4):
                    c = slice(BANK * b, BANK * b + BANK)
                    v.scalar_tensor_tensor(out=accT[:, c], in0=fold4[:, c], scalar=b0[:, :], in1=curT[:, c],
                                           op0=ALU.add, op1=ALU.add).then_inc(acc_taken, 1)
                norm.variances(dve, do)
                norm.scale(dve, do, moved, nat4, x_made)
                dve.wait_ge(x_made, 4)
                v.tensor_copy(res[:, :, :], moved[:, :, :]).then_inc(res_copied, 1)
                dve.wait_ge(deg_ready, 1)
                v.tensor_scalar(blocks4(st["rdeg"]), columns(4), 1.0, None, ALU.max).then_inc(deg_taken, 1)
                dve.wait_ge(deg_taken, 1)
                do(v.reciprocal(st["rdeg"][:, :], st["rdeg"][:, :]))
                dve.wait_ge(fold_ready, 1)
                v.tensor_copy(curT[:, :], fold4b).then_inc(fold_taken, 1)
                dve.wait_ge(self_ready, 1)
                do(v.tensor_copy(cur[:, :, :], nat4b))

            def side(pe):
                pe.wait_ge(rows_taken, 4)
                rows_to_columns(4).then_inc(deg_ready, 1)
                pe.wait_ge(deg_taken, 1)
                fold(moved, fold4b).then_inc(fold_ready, 1)
                pe.wait_ge(fold_taken, 1)
                project(nat4b, curT, w1s).then_inc(self_ready, 1)

            accumulate(block, sem, adjT_b, None, (x_made, 4), (x_made, 4), {3: side},
                       seq=[*range(24, NB), *range(24)], slots=range(8), resident=8)

        with phase("i0_edge") as (block, sem):
            acc_taken, chain, x_ready, nb_ready = (sem(n) for n in
                                                   ("acc_taken", "dve_step", "x_ready", "neighbours_ready"))
            norm = LayerNorm(sem)

            @block.scalar
            def _(act):
                norm.scalar(act, res)

            @block.tensor
            def _(pe):
                pe.wait_ge(acc_taken, 1)
                project(nat4, accT, w1n, nb_ready)

            @block.vector
            def _(dve):
                v = nc.vector
                do = Chain(dve, chain)
                v.tensor_copy(accT[:, :], fold4).then_inc(acc_taken, 1)
                for k in range(4):
                    dve.wait_ge(nb_ready, k + 1)
                    do(v.tensor_tensor(part(tmp, k), part(nat4, k), per_node_part(st["rdeg"], k), ALU.mult))
                    do(v.tensor_tensor(part(cur, k), part(tmp, k), part(cur, k), ALU.add))
                    do(v.scalar_tensor_tensor(out=part(res, k).rearrange("p n f -> p (n f)"),
                                              in0=part(cur, k).rearrange("p n f -> p (n f)"), scalar=0.0,
                                              in1=part(res, k).rearrange("p n f -> p (n f)"),
                                              op0=ALU.max, op1=ALU.add))
                norm.centre(do, res)
                dve.wait_ge(norm.centred, 4)
                norm.variances(dve, do)
                norm.scale(dve, do, res, res, x_ready)

            edge_pass(block, sem, res, [(x_ready, k + 1) for k in range(4)])

        def global_softmax_vector(dve, do, sems):
            v = nc.vector
            v.reduce_max(gl["gmax"][:, :], st["score"][:, :], AX.X).then_inc(sems["part_max"], 1)
            dve.wait_ge(sems["all_max"], 1)
            v.tensor_scalar(gl["gneg"][:, :], gl["gmaxall"][:, :], -1.0, None, ALU.mult)\
                .then_inc(sems["bias_ready"], 1)
            dve.wait_ge(sems["all_sum"], 1)
            do(v.reciprocal(gl["grec"][:, :], gl["gsumall"][:, :]))
            do(v.tensor_scalar(st["score"][:, :], st["score"][:, :], gl["grec"][:, :], None, ALU.mult))

        def global_softmax_pool(pool, sems):
            pool.wait_ge(sems["part_max"], 1)
            nc.gpsimd.partition_all_reduce(gl["gmaxall"][:, :], gl["gmax"][:, :], P,
                                           bass.bass_isa.ReduceOp.max).then_inc(sems["all_max"], 1)
            pool.wait_ge(sems["part_sum"], 1)
            nc.gpsimd.partition_all_reduce(gl["gsumall"][:, :], gl["gsum"][:, :], P,
                                           bass.bass_isa.ReduceOp.add).then_inc(sems["all_sum"], 1)

        def global_softmax_scalar(act, sems):
            act.wait_ge(sems["bias_ready"], 1)
            nc.scalar.activation(st["score"][:, :], st["score"][:, :], ACT.Exp, bias=gl["gneg"][:, :],
                                 accum_out=gl["gsum"][:, :]).then_inc(sems["part_sum"], 1)

        SOFT = ("part_max", "all_max", "bias_ready", "part_sum", "all_sum")
        SL3 = 3
        CHUNK = 2 * BANK
        NC = N // CHUNK
        held = [stream[:, s, :] for s in range(3)]
        prod = [stream[:, 3 + s, :] for s in range(3)]

        def score_products(pe, t, scores_ready, chunk_used, operands):
            for c in range(NC):
                if t.it is None and t.n == 0:
                    for ready in operands:
                        pe.wait_ge(ready, c + 1)
                slot = (NC * t.k + c) % SL3
                wait(pe, chunk_used, t.n * NC + (c - 2))
                for j in range(2):
                    cols = slice(CHUNK * c + BANK * j, CHUNK * c + BANK * j + BANK)
                    rows_n = bass.ds(t.block * P, P)
                    out = ps[:, 2 * slot + j, :]
                    nc.tensor.matmul(out, sta_a[:, rows_n], mov_a[:, cols], start=True, stop=False)
                    nc.tensor.matmul(out, sta_a[:, rows_n], mov_b[:, cols], start=False, stop=False)
                    last = nc.tensor.matmul(out, sta_b[:, rows_n], mov_c[:, cols], start=False, stop=True)
                last.then_inc(scores_ready, 1)

        def weighted_scores(dve, t, block_in, seen, scores_ready, chunk_used, max_ready, between=None):
            s = t.k % SL3
            for c in range(NC):
                slot = (NC * t.k + c) % SL3
                if between and c == NC - 1:
                    between()
                dve.wait_ge(scores_ready, t.n * NC + (c + 1))
                dve.sem_inc(seen, 1)
                cols = slice(CHUNK * c, CHUNK * c + CHUNK)
                nc.vector.tensor_tensor_reduce(
                    out=prod[s][:, cols], in0=ps[:, 2 * slot:2 * slot + 2, :].rearrange("p a b -> p (a b)"),
                    in1=block_in[:, cols], scale=1.0, scalar=NEG_HUGE, op0=ALU.mult, op1=ALU.max,
                    accum_out=mx4[:, s, c:c + 1]).then_inc(chunk_used, 1)
            dve.wait_ge(chunk_used, t.n * NC + NC)
            nc.vector.tensor_reduce(negmax[:, s:s + 1], mx4[:, s, :], AX.X, ALU.max, negate=True)\
                .then_inc(max_ready, 1)

        def exponentials(act, t, max_ready, exp_done):
            s = t.k % SL3
            act.wait_ge(max_ready, t.n + 1)
            nc.scalar.activation(prod[s], prod[s], ACT.Exp, bias=negmax[:, s:s + 1],
                                 accum_out=zsum[:, s:s + 1]).then_inc(exp_done, 1)

        for it in range(2):
            th = THETAS[it]
            last_it = it == 1

            with phase(f"i{it}_attend") as (block, sem):
                loaded = [sem(f"block_loaded{s}") for s in range(SL3)]
                scores_ready, chunk_used, max_ready = sem("scores_ready"), sem("chunk_used"), sem("max_ready")
                seen = sem("scores_seen")
                exp_done, rz_ready, summed = sem("exp_done"), sem("rz_ready"), sem("left_half_summed")
                half_zero, half_scaled, half_added = (sem(n) for n in
                                                      ("half_sum_zero", "right_half_scaled", "right_half_added"))
                half_sum = moved[:, :, :].rearrange("p n f -> p (n f)")
                hi_ready, a_spread, bc_spread, chain = (sem(n) for n in
                                                        ("hi_ready", "mov_a_spread", "mov_bc_spread", "dve_step"))
                seq = [30, 31, 26, 27, 28, 29, *range(26)]
                R, LEAD = 3, 8

                @block.vector
                def _(dve):
                    v = nc.vector
                    do = Chain(dve, chain)
                    for k in range(4):
                        hi_k, rest_k, mid_k, lo_k = (bank_of(x, k) for x in (hi, rest, mid, lo))
                        dve.wait_ge(hi_ready, k + 1)
                        do(v.tensor_tensor(rest_k, bank_of(fold4b, k), hi_k, ALU.subtract))
                        do(v.tensor_copy(mid_k, rest_k))
                        do(v.tensor_tensor(lo_k, rest_k, mid_k, ALU.subtract))
                        spread_bank(v.tensor_copy, mov_b, mid, mid, k)
                        spread_bank(v.tensor_copy, mov_c, lo, hi, k).then_inc(bc_spread, 1)
                    dve.wait_ge(a_spread, 4)
                    dve.wait_ge(bc_spread, 4)

                @block.scalar
                def _(act):
                    for k in range(4):
                        nc.scalar.copy(bank_of(hi, k), bank_of(fold4b, k)).then_inc(hi_ready, 1)
                        act.wait_ge(hi_ready, k + 1)
                        spread_bank(nc.scalar.copy, mov_a, hi, hi, k).then_inc(a_spread, 1)

                @block.sync
                def _(sp):
                    def body(t):
                        if t.k >= R:
                            sp.wait_ge(chunk_used, t.n * NC - (SL3 - 1) * NC)
                            sp.dma_start(held[t.k % SL3], adj_b[t.block]).then_inc(loaded[t.k % SL3], 16)
                    row_blocks(sp, 3, LEAD, body, seq)

                @block.tensor
                def _(pe):
                    def column_sum(t):
                        s = t.k % SL3
                        pe.wait_ge(rz_ready, t.n + 1)
                        for g in range(4):
                            last = nc.tensor.matmul(ps[32 * g:32 * g + 1, 6, :], rz[:, s:s + 1],
                                                    prod[s][:, BANK * g:BANK * g + BANK], start=False,
                                                    stop=False, skip_group_check=True)
                        last.then_inc(summed, 1)

                    def body(t):
                        score_products(pe, t, scores_ready, chunk_used, (a_spread, bc_spread))
                        if t.it is None and t.k == 0:
                            for g in range(4):
                                nc.tensor.matmul(ps[32 * g:32 * g + 1, 6, :], zeros_b[:, 0:1], zeros_b[:, :],
                                                 start=True, stop=False, skip_group_check=True)
                        if t.k >= 2:
                            column_sum(t.back(2))
                    row_blocks(pe, 3, LEAD, body, seq)
                    column_sum(last_step(NB - 2, seq))
                    pe.wait_ge(half_added, NB - 1)
                    for g in range(4):
                        nc.tensor.matmul(ps[32 * g:32 * g + 1, 7, :], ones[:, :], bank_of(half_sum, g),
                                         start=True, stop=False, skip_group_check=True)
                    column_sum(last_step(NB - 1, seq))
                    s = (NB - 1) % SL3
                    for g in range(4):
                        nc.tensor.matmul(ps[32 * g:32 * g + 1, 7, :], rz[:, s:s + 1], bank_of(prod[s], 4 + g),
                                         start=False, stop=True, skip_group_check=True)

                @block.gpsimd
                def _(pool):
                    nc.gpsimd.memset(half_sum, 0.0).then_inc(half_zero, 1)
                    pool.wait_ge(half_zero, 1)

                    def add(t):
                        pool.wait_ge(half_scaled, t.n + 1)
                        wait(pool, half_added, t.n)
                        nc.gpsimd.tensor_tensor(half_sum, prod[t.k % SL3][:, HALF:N], half_sum, ALU.add)\
                            .then_inc(half_added, 1)

                    def body(t):
                        if t.k >= 1:
                            add(t.back(1))
                    row_blocks(pool, 3, LEAD, body, seq)

                @block.vector
                def _(dve):
                    def reciprocal(t):
                        s = t.k % SL3
                        dve.wait_ge(exp_done, t.n + 1)
                        nc.vector.reciprocal(rz[:, s:s + 1], zsum[:, s:s + 1]).then_inc(rz_ready, 1)

                    def body(t):
                        if t.k >= R:
                            dve.wait_ge(loaded[t.k % SL3], 16 * (t.turn(SL3, R) + 1))
                        wait(dve, summed, t.n - 2)
                        wait(dve, half_added, t.n - 2)
                        weighted_scores(dve, t, held[t.k % SL3], seen, scores_ready, chunk_used, max_ready,
                                        (lambda: reciprocal(t.back(1))) if t.k >= 1 else None)
                    row_blocks(dve, 3, LEAD, body, seq)
                    reciprocal(last_step(NB - 1, seq))

                @block.scalar
                def _(act):
                    def scale_right(t):
                        s = t.k % SL3
                        act.wait_ge(rz_ready, t.n + 1)
                        nc.scalar.activation(prod[s][:, HALF:N], prod[s][:, HALF:N], ACT.Copy,
                                             scale=rz[:, s:s + 1]).then_inc(half_scaled, 1)

                    def body(t):
                        if t.k >= 1:
                            scale_right(t.back(1))
                        exponentials(act, t, max_ready, exp_done)
                    row_blocks(act, 3, LEAD, body, seq)

            with phase(f"i{it}_prune") as (block, sem):
                rows_taken, att_ready, chain = sem("rows_taken"), sem("att_ready"), sem("dve_step")
                comp_ready, mask_ready, hi_ready = sem("comp_ready"), sem("mask_ready"), sem("hi_ready")
                a_spread, bc_spread = sem("mov_a_spread"), sem("mov_bc_spread")
                comp_sems = {n: sem("comp_" + n) for n in SOFT}

                @block.scalar
                def _(act):
                    take_rows(nc.scalar.copy, 6, (0, 1), rows_taken)
                    spread_rows(nc.scalar.copy, sta_b, TOP, xn_hi)
                    global_softmax_scalar(act, comp_sems)
                    for k in range(4):
                        act.wait_ge(hi_ready, k + 1)
                        spread_bank(nc.scalar.copy, mov_a, hi, hi, k).then_inc(a_spread, 1)

                @block.gpsimd
                def _(pool):
                    global_softmax_pool(pool, comp_sems)

                @block.tensor
                def _(pe):
                    pe.wait_ge(rows_taken, 4)
                    rows_to_columns(0).then_inc(att_ready, 1)
                    pe.wait_ge(comp_ready, 1)
                    for c in range(HB):
                        for h in range(2):
                            b = 2 * c + h
                            last = nc.tensor.matmul(fold4b[F * h:F * h + F, P * c:P * c + P],
                                                    comp_b[:, b:b + 1].to_broadcast([P, F]), ident_b[:, :],
                                                    start=True, stop=True)
                        if c % 4 == 3:
                            last.then_inc(mask_ready, 1)

                @block.vector
                def _(dve):
                    v = nc.vector
                    do = Chain(dve, chain)
                    take_rows(v.tensor_copy, 6, (2, 3), rows_taken)
                    spread(v.tensor_copy, sta_a, xn_hi, xn_mid)
                    spread_rows(v.tensor_copy, sta_b, LOW, xn_lo)
                    do(v.tensor_scalar(st["score"][:, :], st["struct"][:, :], 0.5, None, ALU.mult))
                    dve.wait_ge(att_ready, 1)
                    do(v.tensor_scalar(blocks4(st["mean"]), columns(0), 0.5 / N, None, ALU.mult))
                    do(v.tensor_tensor(st["score"][:, :], st["mean"][:, :], st["score"][:, :], ALU.add))
                    global_softmax_vector(dve, do, comp_sems)
                    do(v.tensor_scalar(st["comp"][:, :], st["score"][:, :], th, None, ALU.is_ge))
                    v.tensor_copy(comp_b[:, :], st["comp"][:, :]).then_inc(comp_ready, 1)
                    do(v.tensor_scalar(st["refuse"][:, :], st["comp"][:, :], -REFUSE, REFUSE, ALU.mult, ALU.add))
                    do(v.tensor_tensor(st["feat"][:, :], st["norm"][:, :], st["comp"][:, :], ALU.mult))
                    do(v.tensor_scalar(st["feat"][:, :], st["feat"][:, :], FEAT_FLOOR, None, ALU.max))
                    for k in range(4):
                        dve.wait_ge(mask_ready, k + 1)
                        v.tensor_tensor(bank_of(hi, k), bank_of(fold4b, k), bank_of(xn_hi, k), ALU.mult)\
                            .then_inc(hi_ready, 1)
                        v.tensor_tensor(bank_of(mid, k), bank_of(fold4b, k), bank_of(xn_mid, k), ALU.mult)
                        do(v.tensor_tensor(bank_of(lo, k), bank_of(fold4b, k), bank_of(xn_lo, k), ALU.mult))
                        spread_bank(v.tensor_copy, mov_b, mid, mid, k)
                        spread_bank(v.tensor_copy, mov_c, lo, hi, k).then_inc(bc_spread, 1)
                    dve.wait_ge(a_spread, 4)
                    dve.wait_ge(bc_spread, 4)

                loaded = [sem(f"block_loaded{s}") for s in range(SL3)]
                stored = [sem(f"block_stored{s}") for s in range(SL3)]
                scores_ready, chunk_used, max_ready = sem("scores_ready"), sem("chunk_used"), sem("max_ready")
                seen = sem("scores_seen")
                exp_done, cut_ready, pruned = sem("exp_done"), sem("cut_ready"), sem("pruned")
                seq = [23, 24, 25, 26, 27, 28, 29, 30, 31, *range(23)]
                R, LEAD = 3, 11
                gather_seq, gather_slots = [*range(20, NB), *range(20)], (5, 3, 4, 0, 1, 2)
                gather_loaded = [sem(f"row_block_loaded{s}") for s in range(6)]

                def buffer(t):
                    if t.k < R:
                        return held[(t.k + 2) % SL3]
                    return spare_block if t.k == R else held[(t.k + 1) % SL3]

                @block.sync
                def _(sp):
                    def store(t):
                        s = t.k % SL3
                        sp.wait_ge(pruned, t.n + 1)
                        sp.dma_start(Hp_rows[t.block], quarters(prod[s])).then_inc(stored[s], 16)

                    def load(t):
                        sp.dma_start(buffer(t), adj_b[t.block]).then_inc(loaded[t.k % SL3], 16)

                    def body(t):
                        if t.k >= SL3:
                            store(t.back(SL3))
                        if t.k in (3, 4, 5):
                            load(Step(t.n + 1, t.k + 1, None, 3, seq))
                        if t.k >= 7:
                            load(t)
                    load(Step(3, 3, None, 3, seq))
                    row_blocks(sp, 3, LEAD + 3, body, seq)
                    for n in range(NB - SL3, NB):
                        store(last_step(n, seq))
                        step = n - (NB - SL3) + SL3
                        sp.dma_start(quarters(stream[:, gather_slots[step], :]), Hp_rows[gather_seq[step]])\
                            .then_inc(gather_loaded[step], 16)
                    for s in range(SL3):
                        sp.wait_ge(stored[s], 16 * len(range(s, NB, SL3)))

                @block.tensor
                def _(pe):
                    row_blocks(pe, 3, LEAD, lambda t: score_products(pe, t, scores_ready, chunk_used,
                                                                     (a_spread, bc_spread)), seq)

                @block.vector
                def _(dve):
                    def prune(t):
                        s = t.k % SL3
                        dve.wait_ge(exp_done, t.n + 1)
                        nc.vector.scalar_tensor_tensor(
                            out=cut[:, s:s + 1], in0=zsum[:, s:s + 1], scalar=th,
                            in1=st["refuse"][:, bass.ds(t.block, 1)], op0=ALU.mult, op1=ALU.add)\
                            .then_inc(cut_ready, 1)
                        dve.wait_ge(cut_ready, t.n + 1)
                        nc.vector.scalar_tensor_tensor(
                            out=prod[s], in0=prod[s], scalar=cut[:, s:s + 1], in1=buffer(t),
                            op0=ALU.is_ge, op1=ALU.mult,
                            accum_out=st["conn"][:, bass.ds(t.block, 1)]).then_inc(pruned, 1)

                    def body(t):
                        s = t.k % SL3
                        if t.k >= R:
                            dve.wait_ge(loaded[s], 16 * (t.turn(SL3, R) + 1))
                        wait(dve, stored[s], t.turn(SL3) * 16)
                        weighted_scores(dve, t, buffer(t), seen, scores_ready, chunk_used, max_ready)
                        if t.k == 0:
                            prune(t)
                        if t.k >= 2:
                            prune(t.back(1))
                    row_blocks(dve, 3, LEAD, body, seq)
                    prune(last_step(NB - 1, seq))
                    dve.wait_ge(pruned, NB)

                @block.scalar
                def _(act):
                    row_blocks(act, 3, LEAD, lambda t: exponentials(act, t, max_ready, exp_done), seq)

                moved_ready, deg_floor, deg_root = sem("moved_ready"), sem("deg_floor"), sem("deg_root")
                node_chain = sem("node_step")
                node_sems = {n: sem("node_" + n) for n in SOFT}

                @block.scalar
                def _(act):
                    global_softmax_scalar(act, node_sems)
                    act.wait_ge(deg_floor, 1)
                    nc.scalar.activation(st["dv"][:, :], st["dv"][:, :], ACT.Sqrt).then_inc(deg_root, 1)

                @block.gpsimd
                def _(pool):
                    global_softmax_pool(pool, node_sems)

                @block.vector
                def _(dve):
                    v = nc.vector
                    do = Chain(dve, node_chain)
                    v.tensor_scalar(st["dv"][:, :], st["conn"][:, :], DEG_EPS, None, ALU.max).then_inc(deg_floor, 1)
                    do(v.tensor_tensor(st["score"][:, :], st["conn"][:, :], st["feat"][:, :], ALU.mult))
                    global_softmax_vector(dve, do, node_sems)
                    do(v.scalar_tensor_tensor(out=st["node"][:, :], in0=st["score"][:, :], scalar=th,
                                              in1=st["comp"][:, :], op0=ALU.is_ge, op1=ALU.mult))
                    do(v.scalar_tensor_tensor(out=st["node"][:, :], in0=st["conn"][:, :], scalar=0.0,
                                              in1=st["node"][:, :], op0=ALU.is_gt, op1=ALU.mult))
                    dve.wait_ge(deg_root, 1)
                    do(v.reciprocal(st["dv"][:, :], st["dv"][:, :]))
                    do(v.tensor_tensor(st["node"][:, :], st["node"][:, :], st["dv"][:, :], ALU.mult))
                    v.tensor_tensor(moved[:, :, :], xw[:, :, :], per_node(st["node"]), ALU.mult)\
                        .then_inc(moved_ready, 1)

                scatter_ahead = loads_ahead(f"i{it}_scatter")
                accumulate(block, sem, Hp_rows, in_turned_order, (moved_ready, 1), (moved_ready, 1),
                           seq=gather_seq, slots=gather_slots, resident=3, issued=6, loaded=gather_loaded, lead=14,
                           ahead=[(steps, stream[:, n, :], Hp_quarters[n], scatter_ahead[n])
                                  for n, steps in enumerate((28, 29, 30, 32))])

            with phase(f"i{it}_scatter", scatter_ahead) as (block, sem):
                acc_taken, rows_taken, chain = sem("acc_taken"), sem("rows_taken"), sem("dve_step")
                nat_ready, deg_ready, agg_ready = sem("nat_ready"), sem("deg_ready"), sem("agg_ready")
                row_summed, row_mean, centred = sem("row_summed"), sem("row_mean"), sem("centred")
                SL = 4
                loaded = scatter_ahead
                next_ahead = loads_ahead("l3" if last_it else f"i{it + 1}_edge")
                turned_done, msg_ready, msg_taken, out_ready, out_taken = (
                    sem(n) for n in ("turned", "msg_ready", "msg_taken", "out_ready", "out_taken"))
                turned = [stream[:, 4 + s, :] for s in range(2)]

                @block.sync
                def _(sp):
                    def body(t):
                        if t.k < SL:
                            return
                        sp.wait_ge(turned_done, t.n - (SL - 1))
                        sp.dma_start(stream[:, t.k % SL, :], Hp_quarters[t.n]).then_inc(loaded[t.k % SL], 16)
                    row_blocks(sp, 4, 4, body)
                    for s in range(SL):
                        sp.wait_ge(turned_done, NB - SL + 1 + s)
                        sp.dma_start(stream[:, s, :], adj_b[s]).then_inc(next_ahead[s], 16)

                @block.tensor
                def _(pe):
                    pe.wait_ge(rows_taken, 4)
                    rows_to_columns(4).then_inc(deg_ready, 1)
                    pe.wait_ge(acc_taken, 1)
                    unfold(accT, nat4, nat_ready)
                    pe.wait_ge(agg_ready, 1)

                    def gather(t):
                        s = t.k % 2
                        pe.wait_ge(turned_done, t.n + 1)
                        wait(pe, msg_taken, t.n - 1)
                        view = turned[s].rearrange("p (g b r) -> p b g r", g=4, r=32)
                        for b in range(NB):
                            h = b % 2
                            last = nc.tensor.matmul(ps[F * h:F * h + F, 4 + s, 0:P], moved[:, b, :], view[:, b, :, :],
                                                    start=b < 2, stop=b >= NB - 2, skip_group_check=True)
                        last.then_inc(msg_ready, 1)

                    def finish(t):
                        s = t.k % 2
                        pe.wait_ge(msg_taken, t.n + 1)
                        wait(pe, out_taken, t.n - 1)
                        nc.tensor.matmul(ps[:, 6 + s, 0:F], msgT[:, s, :], theta[:, :],
                                         start=True, stop=True).then_inc(out_ready, 1)

                    def body(t):
                        gather(t)
                        if t.k >= 1:
                            finish(t.back(1))
                    row_blocks(pe, 4, 4, body)
                    finish(last_step(NB - 1))

                @block.scalar
                def _(act):
                    take_rows(nc.scalar.copy, 4, (0, 1), rows_taken)

                    def message(t):
                        s = t.k % 2
                        act.wait_ge(msg_ready, t.n + 1)
                        wait(act, out_ready, t.n - 1)
                        by_node = ps[:, 4 + s, 0:P].rearrange("p (g r) -> p r g", g=4)
                        nc.scalar.copy(msgT[:, s, :].rearrange("p (r g) -> p r g", g=4), by_node)\
                            .then_inc(msg_taken, 1)

                    def output(t):
                        s = t.k % 2
                        act.wait_ge(out_ready, t.n + 1)
                        nc.scalar.activation(natural_block(cur, t.n), ps[:, 6 + s, 0:F], ACT.Relu,
                                             scale=st["dv"][:, bass.ds(t.n, 1)]).then_inc(out_taken, 1)

                    def variance(t):
                        act.wait_ge(centred, t.n + 1)
                        nc.scalar.activation(natural_block(tmp, t.n), natural_block(res, t.n), ACT.Square,
                                             accum_out=st["var"][:, bass.ds(t.n, 1)])

                    def body(t):
                        message(t)
                        if t.k >= 1:
                            output(t.back(1))
                        if last_it and t.k >= 4:
                            variance(t.back(4))
                    row_blocks(act, 4, 8 if last_it else 4, body)
                    output(last_step(NB - 1))
                    if last_it:
                        for n in range(NB - 4, NB):
                            variance(last_step(n))

                @block.vector
                def _(dve):
                    v = nc.vector
                    do = Chain(dve, chain)

                    def turn(t):
                        dve.wait_ge(loaded[t.k % SL], 16 * (t.turn(SL) + 1))
                        wait(dve, msg_ready, t.n - 1)
                        v.transpose(turned[t.k % 2], stream[:, t.k % SL, :]).then_inc(turned_done, 1)

                    def residual(t):
                        mean = st["mean"][:, bass.ds(t.n, 1)]
                        dve.wait_ge(out_taken, t.n + 1)
                        v.scalar_tensor_tensor(out=natural_block(res, t.n), in0=natural_block(cur, t.n), scalar=1.0,
                                               in1=natural_block(res, t.n), op0=ALU.mult, op1=ALU.add,
                                               accum_out=mean).then_inc(row_summed, 1)
                        dve.wait_ge(row_summed, t.n + 1)
                        v.tensor_scalar(mean, mean, 1.0 / F, None, ALU.mult).then_inc(row_mean, 1)
                        dve.wait_ge(row_mean, t.n + 1)
                        v.tensor_scalar(natural_block(res, t.n), natural_block(res, t.n), mean, None, ALU.subtract)\
                            .then_inc(centred, 1)

                    take_rows(v.tensor_copy, 4, (2, 3), rows_taken)
                    v.tensor_copy(accT[:, :].rearrange("p (m q i) -> p m q i", q=4, i=32),
                                  fold4.rearrange("p (q m i) -> p m q i", q=4, i=32)).then_inc(acc_taken, 1)
                    dve.wait_ge(deg_ready, 1)
                    do(v.tensor_scalar(blocks4(st["var"]), columns(4), DEG_EPS, None, ALU.max))
                    do(v.reciprocal(st["var"][:, :], st["var"][:, :]))

                    def aggregates():
                        for k in range(4):
                            dve.wait_ge(nat_ready, k + 1)
                            last = v.tensor_tensor(
                                part(moved, k).rearrange("p (h a) f -> p a h f", h=2),
                                part(nat4, k).rearrange("p (a h) f -> p a h f", h=2),
                                part(st["var"], k).rearrange("p (h a) -> p a h", h=2).unsqueeze(3)
                                .to_broadcast([P, 4, 2, F]), ALU.mult)
                        last.then_inc(agg_ready, 1)

                    def body(t):
                        turn(t)
                        if t.it is None and t.k == 0:
                            aggregates()
                        if last_it and t.k >= 3:
                            residual(t.back(3))
                    row_blocks(dve, 4, 4, body)
                    if last_it:
                        for n in range(NB - 3, NB):
                            residual(last_step(n))

            if not last_it:
                with phase(f"i{it + 1}_edge", next_ahead) as (block, sem):
                    cur_ready = sem("cur_ready")

                    @block.vector
                    def _(dve):
                        dve.sem_inc(cur_ready, 1)

                    edge_pass(block, sem, cur, [(cur_ready, 1)] * 4, next_ahead)

        sup_all = streamb[:, 0:3 * HALF].rearrange("p (n t f) -> p n t f", t=3, f=F)
        with phase("l3", next_ahead) as (block, sem):
            x_ready, fold_ready, fold_taken, sup_ready, sup_taken = (
                sem(n) for n in ("x_ready", "fold_ready", "fold_taken", "support_ready", "support_taken"))
            sup_hi, sup_rest, sup_mid, sup_split, biased, chain = (
                sem(n) for n in ("support_hi", "support_rest", "support_mid", "support_split", "biased", "dve_step"))
            norm = LayerNorm(sem)

            @block.scalar
            def _(act):
                norm.root(act)
                act.wait_ge(fold_ready, 1)
                nc.scalar.copy(curT[:, :], fold4b).then_inc(fold_taken, 1)
                act.wait_ge(sup_ready, 1)
                nc.scalar.copy(cur[:, :, :], nat4b).then_inc(sup_taken, 1)
                act.wait_ge(sup_taken, 1)
                nc.scalar.copy(sup_all[:, :, 0, :], cur[:, :, :]).then_inc(sup_hi, 1)

            @block.gpsimd
            def _(pool):
                pool.wait_ge(sup_hi, 1)
                nc.gpsimd.tensor_tensor(cur[:, :, :], cur[:, :, :], sup_all[:, :, 0, :], ALU.subtract)\
                    .then_inc(sup_rest, 1)
                pool.wait_ge(sup_mid, 1)
                nc.gpsimd.tensor_tensor(sup_all[:, :, 2, :], cur[:, :, :], sup_all[:, :, 1, :], ALU.subtract)\
                    .then_inc(sup_split, 1)
                nc.gpsimd.tensor_tensor(res[:, :, :], res[:, :, :], per_feature(b3), ALU.add).then_inc(biased, 1)

            @block.tensor
            def _(pe):
                pe.wait_ge(x_ready, 4)
                fold(res, fold4b).then_inc(fold_ready, 1)
                pe.wait_ge(fold_taken, 1)
                project(nat4b, curT, w3).then_inc(sup_ready, 1)

            @block.vector
            def _(dve):
                do = Chain(dve, chain)
                norm.scale(dve, do, res, res, x_ready)

            SL = 4
            residual_ready, mean_ready, centred = sem("residual_ready"), sem("mean_ready"), sem("out_centred")
            parts_added, parts_seen = sem("parts_added"), sem("parts_seen")
            sums = [stage[:, 3 * s:3 * s + 3, :] for s in range(2)]
            loaded = next_ahead
            masked, scanned, edges = sem("masked"), sem("scanned"), sem("edges_set")
            diff_ready, diff_taken, sum_ready, sum_taken = (sem(n) for n in
                                                            ("diff_ready", "diff_taken", "sum_ready", "sum_taken"))
            factor = [mov_a[:, :], mov_b[:, :]]
            decay = [streamb[:, 3 * HALF + (N + 2) * s:3 * HALF + (N + 2) * s + N + 1] for s in range(2)]
            weight = [mov_c[:, :], sta_a[:, :]]

            @block.sync
            def _(sp):
                def body(t):
                    if t.k < SL:
                        return
                    sp.wait_ge(masked, t.n - (SL - 1))
                    sp.dma_start(stream[:, t.k % SL, :], adj_b[t.n]).then_inc(loaded[t.k % SL], 16)
                row_blocks(sp, 4, 4, body)

            @block.vector
            def _(dve):
                v = nc.vector
                for s in range(2):
                    v.memset(decay[s][:, N:N + 1], 1.0).then_inc(edges, 1)

                def body(t):
                    s = t.k % 2
                    dve.wait_ge(loaded[t.k % SL], 16 * (t.turn(SL) + 1))
                    wait(dve, scanned, t.n - 1)
                    v.tensor_scalar(factor[s], stream[:, t.k % SL, :], 0.0, 0.5, ALU.is_equal, ALU.max)\
                        .then_inc(masked, 1)
                    dve.wait_ge(masked, t.n + 1)
                    wait(dve, diff_ready, t.n * NC - NC)
                    v.tensor_tensor_scan(decay[s][:, N - 1::-1], factor[s][:, ::-1],
                                         floor_w[:, :].to_broadcast([P, N]), 1.0,
                                         ALU.mult, ALU.max).then_inc(scanned, 1)
                row_blocks(dve, 4, 4, body)

            @block.gpsimd
            def _(pool):
                pool.wait_ge(biased, 1)

                def centre(t):
                    pool.wait_ge(mean_ready, t.n + 1)
                    nc.gpsimd.tensor_tensor(natural_block(cur, t.n), natural_block(cur, t.n),
                                            st["mean"][:, bass.ds(t.n, 1)].to_broadcast([P, F]),
                                            ALU.add).then_inc(centred, 1)

                def body(t):
                    out_hi, out_mid, out_lo = (sums[t.k % 2][:, i, :] for i in range(3))
                    pool.wait_ge(sum_taken, t.n + 1)
                    nc.gpsimd.tensor_tensor(natural_block(cur, t.n), out_lo, out_mid, ALU.add).then_inc(parts_added, 1)
                    nc.gpsimd.tensor_tensor(out_hi, out_hi, natural_block(res, t.n), ALU.add).then_inc(parts_added, 1)
                    pool.wait_ge(parts_added, t.n * 2 + 2)
                    pool.sem_inc(parts_seen, 1)
                    nc.gpsimd.tensor_tensor(natural_block(cur, t.n), natural_block(cur, t.n), out_hi, ALU.add)\
                        .then_inc(residual_ready, 1)
                    if t.k >= 1:
                        centre(t.back(1))
                row_blocks(pool, 4, 4, body)
                centre(last_step(NB - 1))

            @block.tensor
            def _(pe):
                pe.wait_ge(edges, 2)

                def combine(t):
                    s = t.k % 2
                    pe.wait_ge(diff_taken, t.n * NC + NC)
                    wait(pe, sum_taken, t.n - 1)
                    for jb in range(NB):
                        last = nc.tensor.matmul(ps[:, 6 + s, 0:3 * F], weight[s][:, P * jb:P * jb + P],
                                                sup_all[:, jb, :, :].rearrange("p t f -> p (t f)"),
                                                start=jb == 0, stop=jb == NB - 1)
                    last.then_inc(sum_ready, 1)

                def body(t):
                    s = t.k % 2
                    pe.wait_ge(scanned, t.n + 1)
                    for q in range(NC):
                        wait(pe, diff_taken, t.n * NC + (q - 1))
                        for i in range(8):
                            jb = 8 * q + i
                            out = ps[:, 2 * (q % 2) + i // 4, P * (i % 4):P * (i % 4) + P]
                            nc.tensor.matmul(out, decay[s][:, P * jb + 1:P * jb + 1 + P], ident_b[:, :],
                                             start=True, stop=False)
                            last = nc.tensor.matmul(out, decay[s][:, P * jb:P * jb + P], neg_ident_b[:, :],
                                                    start=False, stop=True)
                        last.then_inc(diff_ready, 1)
                    if t.it is None and t.k == 1:
                        pe.wait_ge(sup_split, 1)
                    if t.k >= 1:
                        combine(t.back(1))
                row_blocks(pe, 4, 4, body)
                combine(last_step(NB - 1))

            @block.scalar
            def _(act):
                def take_sum(t):
                    act.wait_ge(sum_ready, t.n + 1)
                    wait(act, residual_ready, t.n - 1)
                    nc.scalar.copy(sums[t.k % 2].rearrange("p t f -> p (t f)"), ps[:, 6 + t.k % 2, 0:3 * F])\
                        .then_inc(sum_taken, 1)

                def mean(t):
                    act.wait_ge(residual_ready, t.n + 1)
                    nc.scalar.activation(natural_block(tmp, t.n), natural_block(cur, t.n), ACT.Copy, scale=-1.0 / F,
                                         accum_out=st["mean"][:, bass.ds(t.n, 1)]).then_inc(mean_ready, 1)

                def variance(t):
                    act.wait_ge(centred, t.n + 1)
                    nc.scalar.activation(natural_block(moved, t.n), natural_block(cur, t.n), ACT.Square,
                                         accum_out=st["var"][:, bass.ds(t.n, 1)])

                def body(t):
                    for q in range(NC):
                        act.wait_ge(diff_ready, t.n * NC + (q + 1))
                        wait(act, sum_ready, t.n - 1)
                        nc.scalar.copy(weight[t.k % 2][:, CHUNK * q:CHUNK * q + CHUNK],
                                       ps[:, 2 * (q % 2):2 * (q % 2) + 2, :].rearrange("p a b -> p (a b)"))\
                            .then_inc(diff_taken, 1)
                    if t.k >= 2:
                        take_sum(t.back(2))
                    if t.k >= 4:
                        mean(t.back(4))
                        if t.k >= 5:
                            variance(t.back(5))
                    if t.it is None and t.k == 0:
                        act.wait_ge(sup_rest, 1)
                        nc.scalar.copy(sup_all[:, :, 1, :], cur[:, :, :]).then_inc(sup_mid, 1)
                row_blocks(act, 4, 8, body)
                take_sum(last_step(NB - 2))
                take_sum(last_step(NB - 1))
                for n in range(NB - 4, NB):
                    mean(last_step(n))
                    variance(last_step(n - 1))
                variance(last_step(NB - 1))

        with phase("out") as (block, sem):
            chain, out_stored, out_made = sem("dve_step"), sem("out_stored"), sem("out_made")
            norm = LayerNorm(sem)

            @block.scalar
            def _(act):
                norm.root(act)

            @block.vector
            def _(dve):
                do = Chain(dve, chain)
                norm.scale(dve, do, cur, cur, out_made)

            @block.sync
            def _(sp):
                for k in range(4):
                    sp.wait_ge(out_made, k + 1)
                    sp.dma_start(part(d["out"], k), part(cur, k)).then_inc(out_stored, 16)
                sp.wait_ge(out_stored, 64)


def kernel(**inputs):
    import numpy as np
    import concourse.bacc as bacc
    from concourse.bass_utils import run_bass_kernel_spmd as run

    nc = bacc.Bacc("TRN2", target_bir_lowering=False, num_devices=1)
    adj = np.asarray(inputs["adj"])
    x = np.asarray(inputs["x"])
    arrays = {
        "x": x.reshape(NB, P, F).transpose(1, 0, 2), "xT": x.T, "adj": adj, "adjT": adj.T,
        "W0": inputs["L0_gnn_W"], "b0": inputs["L0_gnn_b"], "W1T": np.asarray(inputs["L1_gnn_W"]).T,
        "W": inputs["L2_gnn_W"], "Theta": inputs["L2_gnn_Theta"], "Wq": inputs["L2_gnn_Wq"],
        "bq": inputs["L2_gnn_bq"], "Wv": inputs["L2_gnn_Wv"], "bv": inputs["L2_gnn_bv"],
        "W3": inputs["L3_gnn_weight"], "b3": inputs["L3_gnn_bias"],
    }
    arrays = {n: np.ascontiguousarray(a) for n, a in arrays.items()}
    d = {n: nc.dram_tensor(f"in_{n}", a.shape, F32, kind="ExternalInput").ap() for n, a in arrays.items()}
    d["out"] = nc.dram_tensor("out", (P, NB, F), F32, kind="ExternalOutput").ap()
    build(nc, d)
    r = run(nc, [{f"in_{n}": a for n, a in arrays.items()}], core_ids=[0])
    return r.results[0]["out"].transpose(1, 0, 2).reshape(N, F)
```
